# Optimizing a Trainium2 kernel written in Bass

```python
import numpy as np
import jax
import jax.numpy as jnp

def _softmax(x, axis=-1):
    return jax.nn.softmax(x, axis=axis)

def _gelu(x):
    return jax.nn.gelu(x, approximate=True)

def _silu(x):
    return jax.nn.silu(x)

def _sigmoid(x):
    return jax.nn.sigmoid(x)

def _layernorm(x, axis=-1, eps=1e-05):
    m = jnp.mean(x, axis=axis, keepdims=True)
    v = jnp.var(x, axis=axis, keepdims=True)
    return (x - m) / jnp.sqrt(v + eps)

def _scatter_add(tgt, idx, src, axis=0):
    return tgt.at[idx].add(src)

def _segment_sum(src, seg, n):
    return jax.ops.segment_sum(src, seg, n)
kernel_name = 'mk_gnn_resnorm_d1_gnn_r8_c4f119'

def setup_inputs(seed: int=0):
    np.random.seed(seed)
    _w = jnp.asarray

    def _rec_inputs():
        import jax
        import jax.numpy as jnp
        _gk = jax.random.key(seed)
        x = -0.000202 + 1 * jax.random.normal(jax.random.fold_in(_gk, 1), (12500, 128), jnp.float32)
        src = jax.random.randint(jax.random.fold_in(_gk, 2), (400000,), 0, 12500, jnp.int32)
        dst = jax.random.randint(jax.random.fold_in(_gk, 3), (400000,), 0, 12500, jnp.int32)
        _o = jnp.argsort(dst, stable=True)
        src = src[_o]
        dst = dst[_o]
        return (x, src, dst)
    x, src, dst = _rec_inputs()

    def _L0_gnn_setup():
        import jax, jax.numpy as jnp
        import numpy as np
        N_NODES = 6250
        N_EDGES = 75000
        D_IN = 128
        D_OUT = 128
        key = jax.random.key(seed)
        k1, k2, k3, k4 = jax.random.split(key, 4)
        x = jax.random.normal(k1, (N_NODES, D_IN), dtype=jnp.float32)
        edge_index = jax.random.randint(k2, (2, N_EDGES), 0, N_NODES, dtype=jnp.int64)
        W1 = jax.random.normal(k3, (2 * D_IN, D_OUT), dtype=jnp.float32) * (1.0 / np.sqrt(2 * D_IN))
        b1 = jnp.zeros((D_OUT,), dtype=jnp.float32)
        W2 = jax.random.normal(k4, (D_OUT, D_OUT), dtype=jnp.float32) * (1.0 / np.sqrt(D_OUT))
        b2 = jnp.zeros((D_OUT,), dtype=jnp.float32)
        return {'x': x, 'edge_index': edge_index, 'W1': W1, 'b1': b1, 'W2': W2, 'b2': b2}
    _L0_gnn_all = _L0_gnn_setup()
    _L0_gnn_in = {k: v for k, v in _L0_gnn_all.items() if k in ('W1', 'b1', 'W2', 'b2')}
    del _L0_gnn_all
    return {'x': x, 'src': src, 'dst': dst, 'L0_gnn_W1': _L0_gnn_in['W1'], 'L0_gnn_b1': _L0_gnn_in['b1'], 'L0_gnn_W2': _L0_gnn_in['W2'], 'L0_gnn_b2': _L0_gnn_in['b2']}

def reference(x, src, dst, L0_gnn_W1, L0_gnn_b1, L0_gnn_W2, L0_gnn_b2):
    import jax
    import jax.numpy as jnp

    def _L0_gnn_ref(x, edge_index, W1, b1, W2, b2):
        import jax, jax.numpy as jnp
        import numpy as np
        N_NODES = 6250
        N_EDGES = 75000
        D_IN = 128
        D_OUT = 128
        row, col = (edge_index[0], edge_index[1])
        x_col = x[col]
        feat = jnp.concatenate([x_col, x[row] - x_col], axis=-1)
        h = jax.nn.relu(feat @ W1 + b1)
        messages = h @ W2 + b2
        out = jax.ops.segment_max(messages, col, num_segments=x.shape[0])
        out = jnp.where(jnp.isneginf(out), jnp.zeros_like(out), out)
        return out
    edge_index = jnp.stack([src, dst])
    x = _layernorm(x + _L0_gnn_ref(x, edge_index, L0_gnn_W1, L0_gnn_b1, L0_gnn_W2, L0_gnn_b2), axis=-1)
    return x

_drawn_inputs = setup_inputs


def setup_inputs(seed=0):
    import zlib

    import numpy as np

    out = dict(_drawn_inputs(seed))
    spreads = {'L0_gnn_b1': (0.0, 0.1), 'L0_gnn_b2': (0.0, 0.1)}
    factors = {}
    for name, (base, spread) in spreads.items():
        noise = np.random.default_rng([zlib.crc32(name.encode()), seed]).standard_normal(out[name].shape)
        drawn = base * np.exp(spread * noise) if base else spread * noise
        out[name] = jnp.asarray(drawn.astype(out[name].dtype))
    for name, factor in factors.items():
        out[name] = (out[name] * factor).astype(out[name].dtype)
    return out
```

```python
from contextlib import ExitStack

import concourse.bass as bass
from concourse import mybir

F32 = mybir.dt.float32
BF16 = mybir.dt.bfloat16
I32 = mybir.dt.int32
U32 = mybir.dt.uint32
I16 = mybir.dt.int16
ALU = mybir.AluOpType
ACT = mybir.ActivationFunctionType
AX = mybir.AxisListType

RING = 4
HALF_BIG = 255.0 * 2.0 ** 119
EPS = 1e-5


def gnn_max_resnorm(nc, x, src, dst, W1, b1, W2, b2, out):
    N, D = x.shape
    E = src.shape[0]

    NP = 125
    KB = N // NP
    assert N == NP * KB and D == 128
    T = 4
    CH = 128 * T
    NC = -(-E // CH)
    LAST = (E - (NC - 1) * CH) // 128
    assert E % 128 == 0 and 1 <= LAST <= T
    LOOPS = (NC - 4) // RING
    GROUP = 5
    assert KB % 4 == 0 and KB % (2 * GROUP) == 0
    WIN = 128
    TOP = N - WIN
    SPAN = 640
    SAMPLES = E // SPAN
    assert SAMPLES * SPAN == E
    G = -(-NC // 128)
    GF = (NC - 1) // 128
    QF = NC - 1 - 128 * GF

    with ExitStack() as ctx:
        def sb(name, shape, dt=F32):
            return ctx.enter_context(nc.sbuf_tensor(name, shape, dt))

        def ps(name):
            return ctx.enter_context(nc.psum_tensor(name, [128, 512], F32))

        def sem(name):
            return ctx.enter_context(nc.semaphore(name))

        def sems(name, n=RING):
            return [sem(f"{name}{i}") for i in range(n)]

        def dram(name, shape, dt=F32):
            return nc.dram_tensor(name, shape, dt, kind="Internal").ap()

        q_tab = dram("q_tab", [N, D])
        p_tab = dram("p_tab", [N, D])
        seg_tab = dram("seg_tab", [E, D])
        row_tab = dram("row_tab", [NC, 2, CH], BF16)
        base_tab = dram("base_tab", [NC, 1], I32)
        flag_tab = dram("flag_tab", [1, 1], I32)
        end_tab = dram("end_tab", [N + 1])

        ident = sb("ident", [128, 128])
        lane_i = sb("lane_i", [128, 1], I32)
        lane = sb("lane", [128, 1])
        node_i = sb("node_i", [NP, KB], I32)
        node = sb("node", [NP, KB])
        ones_row = sb("ones_row", [1, 128])
        ones_bf = sb("ones_bf", [1, 128], BF16)
        zero1 = sb("zero1", [1, 1])
        eps = sb("eps", [NP, 1])
        w1 = sb("w1", [D, 2, D])
        w_qp = sb("w_qp", [D, 2, D])
        w2 = sb("w2", [D, D])
        b1_all = sb("b1_all", [NP, D])
        b2_all = sb("b2_all", [NP, D])
        x_in = sb("x_in", [NP, 2, 2, D])
        x_t = sb("x_t", [D, 2, 2, NP])
        q_out = sb("q_out", [NP, 2, 2, D])
        p_out = sb("p_out", [NP, 2, 2, D])
        dst_c = sb("dst_c", [128, G, CH], I32)
        dst_f = sb("dst_f", [128, G, CH])
        prev_c = sb("prev_c", [128, G], I32)
        prev_f = sb("prev_f", [128, G])
        same = sb("same", [128, G, CH])
        local = sb("local", [128, G, CH])
        row_c = sb("row_c", [128, G, 2, CH], BF16)
        base_f = sb("base_f", [128, G])
        base_i = sb("base_i", [128, G], I32)
        far = sb("far", [128, 1])
        far1 = sb("far1", [1, 1])
        far_i = sb("far_i", [1, 1], I32)
        sample_i = sb("sample_i", [1, SAMPLES], I32)
        sample_f = sb("sample_f", [1, SAMPLES])
        sample_all = sb("sample_all", [NP, SAMPLES])
        junk = sb("junk", [NP, SPAN], BF16)
        coarse = sb("coarse", [NP, KB])
        span_f = sb("span_f", [NP, KB])
        span_at = sb("span_at", [NP, 2, GROUP], U32)
        span_rows = sb("span_rows", [NP, 2, GROUP, SPAN], I32)
        fine = sb("fine", [NP, KB])
        end = sb("end", [NP, KB])
        start = sb("start", [NP, KB])
        filled = sb("filled", [NP, KB])
        last_f = sb("last_f", [NP, KB])
        idx = sb("idx", [128, RING, T], I32)
        idx_d = sb("idx_d", [128, RING, T], I32)
        rows = sb("rows", [1, RING, 2, CH], BF16)
        win = sb("win", [WIN, RING, D])
        q_rows = sb("q_rows", [128, RING, T, D])
        p_rows = sb("p_rows", [128, RING, T, D])
        pick = sb("pick", [WIN, 2, CH])
        limit = sb("limit", [128, RING, CH])
        hid = sb("hid", [D, 2, CH])
        seg = sb("seg", [D, RING, CH])
        seg_t = sb("seg_t", [128, 2, T, D])
        last_at = sb("last_at", [NP, 2, GROUP], U32)
        top = sb("top", [NP, 2, GROUP, D])
        x_r = sb("x_r", [NP, 2, GROUP, D])
        res = sb("res", [NP, 2, GROUP, D])
        stats = sb("stats", [NP, 2, GROUP, 6])
        mv = sb("mv", [NP, 2, GROUP, 2])
        std = sb("std", [NP, 2, GROUP, 1])
        rstd = sb("rstd", [NP, 2, GROUP, 1])
        fin = sb("fin", [NP, 2, GROUP, D])

        ps_local = ps("ps_local")
        ps_limit = ps("ps_limit")
        ps_hid = [ps("ps_hid0"), ps("ps_hid1")]
        ps_msg = [ps("ps_msg0"), ps("ps_msg1")]
        ps_seg = [ps("ps_seg0"), ps("ps_seg1")]

        ident_zeroed, ident_made, iota_made, const_made = (sem("ident_zeroed"), sem("ident_made"),
                                                           sem("iota_made"), sem("const_made"))
        w1_in, w2_in, b1_in, b2_in, w_made = sem("w1_in"), sem("w2_in"), sem("b1_in"), sem("b2_in"), sem("w_made")
        x_loaded = sems("x_loaded", 2)
        xt_made, xt_copied, qp_made = sem("xt_made"), sem("xt_copied"), sem("qp_made")
        q_copied, p_copied = sem("q_copied"), sem("p_copied")
        q_stored, p_stored = sems("q_stored", 2), sems("p_stored", 2)
        dst_zeroed, dst_in, prev_in, sample_in = sem("dst_zeroed"), sem("dst_in"), sem("prev_in"), sem("sample_in")
        dve_step = sem("dve_step")
        rows_made, rows_stored = sem("rows_made"), sem("rows_stored")
        far_made, far_turned, flag_made, flag_stored = (sem("far_made"), sem("far_turned"), sem("flag_made"),
                                                        sem("flag_stored"))
        sample_cast, sample_spread, coarse_made = sem("sample_cast"), sem("sample_spread"), sem("coarse_made")
        span_named, span_in, fine_made = sem("span_named"), sems("span_in", 2), sem("fine_made")
        zero_stored, end_made, end_stored, start_in = (sem("zero_stored"), sem("end_made"), sem("end_stored"),
                                                       sem("start_in"))

        idx_in, rows_in, win_in, gathered = sems("idx_in"), sems("rows_in"), sems("win_in"), sems("gathered")
        spread, picked, limit_copied = sems("spread"), sems("picked"), sems("limit_copied")
        summed, relued, product, scanned = sems("summed"), sems("relued"), sems("product"), sems("scanned")
        turned, turned_copied, seg_stored = sems("turned"), sems("turned_copied"), sems("seg_stored")

        last_named, top_in, x_again = sem("last_named"), sems("top_in", 2), sems("x_again", 2)
        top_b2, top_kept, res_made, stats_made, mv_made = (sem("top_b2"), sem("top_kept"), sem("res_made"),
                                                           sem("stats_made"), sem("mv_made"))
        std_made, rstd_made, fin_made, out_stored = (sem("std_made"), sem("rstd_made"), sem("fin_made"),
                                                     sems("out_stored", 2))

        ctx.enter_context(nc.allow_non_contiguous_dma(reason="one dst for each chunk or span"))
        passed = sem("passed")

        block = ctx.enter_context(nc.Block())

        def wait(eng, stage, i, off, by=1):
            value = (i + off // RING + 1) * by
            if isinstance(value, int) and value <= 0:
                return
            eng.wait_ge(stage[off % RING], value)

        def tiles(off, peeled):
            return LAST if peeled and off == NC - 1 else T

        def chunks(eng, step, ahead=0):
            for s in range(-ahead, RING):
                step(0, s, True)
            with eng.Fori(1, LOOPS) as i:
                for off in range(RING):
                    step(i, off, False)
            for s in range(LOOPS * RING, NC):
                step(0, s, True)

        def turns(eng, n, body):
            for h in range(2):
                body(0, h)
            with eng.Fori(1, n) as i:
                for h in range(2):
                    body(i, h)

        def freed(eng, semaphore, value):
            if not isinstance(value, int) or value > 0:
                eng.wait_ge(semaphore, value)

        def there(off, peeled):
            return not peeled or 0 <= off < NC

        def either(eng, make):
            eng.wait_ge(flag_stored, 16)
            general = eng.value_load(flag_tab[0:1, 0:1], min_val=0, max_val=1)
            with eng.If(general == 0):
                make(False)
            with eng.Else():
                make(True)

        def apart(eng):
            eng.sem_inc(passed, 1)

        def blocks_of(table):
            return table.rearrange("(p k) f -> p k f", k=KB)

        @block.sync
        def _(sp):
            sp.dma_start(w1[:, :, :], W1.rearrange("(a f) o -> f a o", a=2)).then_inc(w1_in, 16)
            sp.dma_start(b1_all[:, :], b1.partition_broadcast(NP)).then_inc(b1_in, 16)

            def load_x(i, h):
                freed(sp, xt_made, 2 * i)
                sp.dma_start(x_in[:, h, :, :], blocks_of(x)[:, bass.ds(4 * i + 2 * h, 2), :]).then_inc(x_loaded[h], 16)

            turns(sp, KB // 4, load_x)
            sp.wait_ge(dst_zeroed, 2)
            sp.dma_start(dst_c[:, 0:GF, :],
                         dst[0:GF * 128 * CH].rearrange("(g q j) -> q g j", q=128, j=CH)).then_inc(dst_in, 16)
            sp.dma_start(dst_c[0:QF, GF, :],
                         dst[GF * 128 * CH:(NC - 1) * CH].rearrange("(q j) -> q j", j=CH)).then_inc(dst_in, 16)
            sp.dma_start(dst_c[QF:QF + 1, GF, 0:LAST * 128],
                         dst[(NC - 1) * CH:E].rearrange("(q j) -> q j", q=1)).then_inc(dst_in, 16)
            ends = dst.rearrange("(e a) -> e a", a=1)
            for g in range(G):
                lo, n = (1 if g == 0 else 0), (128 if g < GF else QF + 1)
                first = (128 * g + lo) * CH - 1
                sp.dma_start(prev_c[lo:n, g:g + 1],
                             ends[first:first + (n - lo - 1) * CH + 1:CH, :]).then_inc(prev_in, 16)
            sp.dma_start(sample_i[:, :], dst.rearrange("(a s j) -> a s j", a=1, j=SPAN)[:, :, 0]).then_inc(sample_in, 16)
            sp.dma_start(w2[:, :], W2).then_inc(w2_in, 16)
            sp.dma_start(b2_all[:, :], b2.partition_broadcast(NP)).then_inc(b2_in, 16)
            sp.wait_ge(const_made, 4)
            sp.dma_start(end_tab[0:1].rearrange("(a b) -> a b", a=1), zero1[:, :]).then_inc(zero_stored, 16)

            sp.wait_ge(rows_made, 1)
            sp.dma_start(row_tab[0:GF * 128].rearrange("(g q) n j -> q g (n j)", q=128),
                         row_c[:, 0:GF].rearrange("q g n j -> q g (n j)")).then_inc(rows_stored, 16)
            sp.dma_start(row_tab[GF * 128:NC].rearrange("q n j -> q (n j)"),
                         row_c[0:QF + 1, GF].rearrange("q n j -> q (n j)")).then_inc(rows_stored, 16)
            for g in range(G):
                n = 128 if g < GF else QF + 1
                sp.dma_start(base_tab[128 * g:128 * g + n, :], base_i[0:n, g:g + 1]).then_inc(rows_stored, 16)
            sp.wait_ge(flag_made, 1)
            sp.dma_start(flag_tab[:, :], far_i[:, :]).then_inc(flag_stored, 16)
            sp.wait_ge(rows_stored, 16 * (2 + G))
            sp.wait_ge(end_made, 1)
            sp.dma_start(end_tab[1:N + 1].rearrange("(p k) -> p k", k=KB), end[:, :]).then_inc(end_stored, 16)
            sp.wait_ge(end_stored, 16)
            sp.wait_ge(zero_stored, 16)
            sp.dma_start(start[:, :], end_tab[0:N].rearrange("(p k) -> p k", k=KB)).then_inc(start_in, 16)
            for h in range(2):
                sp.wait_ge(p_stored[h], 16 * (KB // 4))

            def make(general):
                def load(i, off, peeled):
                    b, nt = off % RING, tiles(off, peeled)
                    at = CH * RING * i + CH * off
                    wait(sp, gathered, i, off - RING, 16 * T * (2 if general else 1))
                    sp.dma_start(idx[:, b, 0:nt],
                                 src[bass.ds(at, 128 * nt)].rearrange("(p t) -> p t", t=nt)).then_inc(idx_in[b], 16)
                    if general:
                        sp.dma_start(idx_d[:, b, 0:nt],
                                     dst[bass.ds(at, 128 * nt)].rearrange("(p t) -> p t", t=nt)).then_inc(idx_in[b], 16)
                    wait(sp, spread, i, off - RING)
                    sp.dma_start(rows[:, b, :, :], row_tab[bass.ds(RING * i + off, 1), :, :]).then_inc(rows_in[b], 16)
                    if not general:
                        first = sp.value_load(base_tab[bass.ds(RING * i + off, 1), 0:1], min_val=0, max_val=TOP)
                        wait(sp, summed, i, off - RING)
                        sp.dma_start(win[:, b, :], p_tab[bass.ds(first, WIN), :]).then_inc(win_in[b], 16)

                def step(i, off, peeled):
                    if there(off + RING, peeled):
                        load(i, off + RING, peeled)
                    if there(off, peeled):
                        b, nt = off % RING, tiles(off, peeled)
                        wait(sp, turned_copied, i, off)
                        sp.dma_start(seg_tab[bass.ds(CH * RING * i + CH * off, 128 * nt), :]
                                     .rearrange("(p t) f -> p t f", t=nt),
                                     seg_t[:, off % 2, 0:nt, :]).then_inc(seg_stored[b], 16)

                chunks(sp, step, ahead=RING)

            either(sp, make)

            def finish(i, h):
                freed(sp, res_made, 2 * i)
                sp.dma_start(x_r[:, h, :, :],
                             blocks_of(x)[:, bass.ds(GROUP * (2 * i + h), GROUP), :]).then_inc(x_again[h], 16)
                sp.wait_ge(fin_made, 2 * i + h + 1)
                sp.dma_start(blocks_of(out)[:, bass.ds(GROUP * (2 * i + h), GROUP), :],
                             fin[:, h, :, :]).then_inc(out_stored[h], 16)

            turns(sp, KB // GROUP // 2, finish)
            for h in range(2):
                sp.wait_ge(out_stored[h], 16 * (KB // GROUP // 2))

        @block.gpsimd
        def _(pool):
            pool.memset(ident[:, :], 0.0).then_inc(ident_zeroed, 1)
            pool.wait_ge(ident_zeroed, 1)
            pool.affine_select(out=ident[:, :], in_=ident[:, :], compare_op=ALU.not_equal, fill=1.0, base=0,
                               pattern=[[-1, 128]], channel_multiplier=1).then_inc(ident_made, 1)
            pool.iota(lane_i[:, :], pattern=[[0, 1]], base=0, channel_multiplier=1).then_inc(iota_made, 1)
            pool.iota(node_i[:, :], pattern=[[1, KB]], base=0, channel_multiplier=KB).then_inc(iota_made, 1)

            spans = dst.rearrange("(s j) -> s j", j=SPAN)

            def fetch_spans(i, h):
                pool.wait_ge(span_named, 2 * i + h + 1)
                apart(pool)
                for k in range(GROUP):
                    pool.indirect_dma_start(
                        out=span_rows[:, h, k, :], out_offset=None, in_=spans,
                        in_offset=bass.IndirectOffsetOnAxis(ap=span_at[:, h, k:k + 1], axis=0)
                    ).then_inc(span_in[h], 16)

            turns(pool, KB // GROUP // 2, fetch_spans)

            for h in range(2):
                pool.wait_ge(q_stored[h], 16 * (KB // 4))
                pool.wait_ge(p_stored[h], 16 * (KB // 4))

            def make(general):
                def step(i, off, peeled):
                    b = off % RING
                    wait(pool, idx_in, i, off, 32 if general else 16)
                    wait(pool, summed, i, off - RING)
                    apart(pool)
                    for rows_of, table, at in ((q_rows, q_tab, idx), (p_rows, p_tab, idx_d))[0:2 if general else 1]:
                        for t in range(tiles(off, peeled)):
                            pool.indirect_dma_start(
                                out=rows_of[:, b, t, :], out_offset=None, in_=table,
                                in_offset=bass.IndirectOffsetOnAxis(ap=at[:, b, t:t + 1].bitcast(U32), axis=0)
                            ).then_inc(gathered[b], 16)

                chunks(pool, step)

            either(pool, make)
            for c in range(NC - RING, NC):
                wait(pool, seg_stored, 0, c, 16)

            def fetch_tops(i, h):
                pool.wait_ge(last_named, 2 * i + h + 1)
                apart(pool)
                for k in range(GROUP):
                    pool.indirect_dma_start(
                        out=top[:, h, k, :], out_offset=None, in_=seg_tab,
                        in_offset=bass.IndirectOffsetOnAxis(ap=last_at[:, h, k:k + 1], axis=0)
                    ).then_inc(top_in[h], 16)

            turns(pool, KB // GROUP // 2, fetch_tops)

        @block.scalar
        def _(act):
            def to_tables(i, h):
                    act.wait_ge(xt_made, 2 * i + h + 1)
                    freed(act, qp_made, 2 * i)
                    act.activation(x_t[:, h, :, :], ps_hid[h][:, 0:2 * NP].rearrange("f (k n) -> f k n", k=2),
                                   ACT.Copy).then_inc(xt_copied, 1)
                    act.wait_ge(qp_made, 2 * i + h + 1)
                    freed(act, q_stored[h], 16 * i)
                    act.activation(q_out[:, h, :, :], ps_msg[h][0:NP, 0:2 * D].rearrange("n (k f) -> n k f", k=2), ACT.Copy).then_inc(q_copied, 1)
                    act.wait_ge(q_copied, 2 * i + h + 1)
                    act.dma_start(blocks_of(q_tab)[:, bass.ds(4 * i + 2 * h, 2), :], q_out[:, h, :, :]).then_inc(q_stored[h], 16)
                    act.wait_ge(p_copied, 2 * i + h + 1)
                    act.dma_start(blocks_of(p_tab)[:, bass.ds(4 * i + 2 * h, 2), :], p_out[:, h, :, :]).then_inc(p_stored[h], 16)

            turns(act, KB // 4, to_tables)

            def make(general):
                def step(i, off, peeled):
                    if there(off + 3, peeled):
                        o = off + 3
                        wait(act, spread, i, o)
                        wait(act, scanned, i, o - RING)
                        act.activation(limit[:, o % RING, :], ps_limit[:, :], ACT.Copy,
                                       scale=2.0).then_inc(limit_copied[o % RING], 1)
                    if there(off + 2, peeled):
                        o = off + 2
                        nt = tiles(o, peeled)
                        wait(act, summed, i, o)
                        wait(act, product, i, o - 2)
                        act.activation(hid[:, o % 2, 0:128 * nt].rearrange("f (p t) -> f p t", t=nt),
                                       ps_hid[o % 2][:, 0:128 * nt].rearrange("f (t p) -> f p t", t=nt),
                                       ACT.Relu).then_inc(relued[o % RING], 1)
                    if there(off, peeled):
                        nt = tiles(off, peeled)
                        wait(act, turned, i, off)
                        wait(act, seg_stored, i, off - 2, 16)
                        act.activation(seg_t[:, off % 2, 0:nt, :],
                                       ps_seg[off % 2][:, 0:128 * nt].rearrange("p (t f) -> p t f", t=nt),
                                       ACT.Copy).then_inc(turned_copied[off % RING], 1)

                chunks(act, step, ahead=3)

            either(act, make)
            with act.Fori(0, KB // GROUP // 2) as i:
                for h in range(2):
                    act.wait_ge(mv_made, 2 * i + h + 1)
                    act.activation(std[:, h, :, :], mv[:, h, :, 1:2], ACT.Sqrt, bias=eps[:, 0:1]).then_inc(std_made, 1)

        @block.tensor
        def _(pe):
            pe.wait_ge(ident_made, 1)
            pe.wait_ge(w_made, 2)
            def products(i, h):
                    pe.wait_ge(x_loaded[h], 16 * i + 16)
                    freed(pe, xt_copied, 2 * i)
                    for k in range(2):
                        mm = pe.transpose(ps_hid[h][:, NP * k:NP * k + NP], x_in[:, h, k, :], ident[0:NP, 0:NP])
                    mm.then_inc(xt_made, 1)
                    pe.wait_ge(xt_copied, 2 * i + h + 1)
                    freed(pe, q_copied, 2 * i)
                    freed(pe, p_copied, 2 * i)
                    for k in range(2):
                        for a, bank in enumerate((ps_msg[h], ps_seg[h])):
                            mm = pe.matmul(bank[0:NP, D * k:D * k + D], x_t[:, h, k, :], w_qp[:, a, :],
                                           start=True, stop=True)
                    mm.then_inc(qp_made, 1)

            turns(pe, KB // 4, products)

            pe.wait_ge(far_made, 1)
            pe.wait_ge(xt_copied, KB // 2)
            pe.transpose(ps_hid[0][0:1, 0:128], far[:, 0:1], ident[:, :]).then_inc(far_turned, 1)
            pe.wait_ge(sample_cast, 1)
            pe.wait_ge(const_made, 4)
            pe.wait_ge(q_copied, KB // 2)
            pe.wait_ge(p_copied, KB // 2)
            for h, (lo, n) in enumerate(((0, 512), (512, SAMPLES - 512))):
                mm = pe.matmul(ps_msg[h][0:NP, 0:n], ones_row[0:1, 0:NP], sample_f[0:1, lo:lo + n], start=True, stop=True)
            mm.then_inc(sample_spread, 1)
            pe.wait_ge(w2_in, 16)
            pe.wait_ge(coarse_made, 1)
            pe.wait_ge(flag_made, 1)

            def make(general):
                def step(i, off, peeled):
                    if there(off + 3, peeled):
                        o = off + 3
                        wait(pe, rows_in, i, o, 16)
                        if not general:
                            wait(pe, picked, i, o - 1)
                            pe.matmul(ps_local[:, :], ones_bf[0:1, :], rows[0:1, o % RING, 1, :], start=True, stop=True)
                        wait(pe, limit_copied, i, o - 1)
                        pe.matmul(ps_limit[:, :], ones_bf[0:1, :], rows[0:1, o % RING, 0, :],
                                  start=True, stop=True).then_inc(spread[o % RING], 1)
                    if there(off + 2, peeled):
                        o = off + 2
                        b, nt = o % RING, tiles(o, peeled)
                        wait(pe, relued, i, o - 2)
                        if peeled and nt < T:
                            pe.wait_ge(gathered[b], 16 * (2 if general else 1) * (T * (o // RING) + nt))
                        else:
                            wait(pe, gathered, i, o, 16 * T * (2 if general else 1))
                        for t in range(nt):
                            pe.matmul(ps_hid[o % 2][:, 128 * t:128 * t + 128], q_rows[:, b, t, :], ident[:, :],
                                      start=(t == 0), stop=False, is_transpose=True, skip_group_check=True)
                        if general:
                            for t in range(nt):
                                mm = pe.matmul(ps_hid[o % 2][:, 128 * t:128 * t + 128], p_rows[:, b, t, :], ident[:, :],
                                               start=False, stop=(t == nt - 1), skip_group_check=True)
                        else:
                            wait(pe, win_in, i, o, 16)
                            wait(pe, picked, i, o)
                            mm = pe.matmul(ps_hid[o % 2][:, 0:128 * nt], win[:, b, :], pick[:, o % 2, 0:128 * nt],
                                           start=False, stop=True, skip_group_check=True)
                        mm.then_inc(summed[b], 1)
                    if there(off + 1, peeled):
                        o = off + 1
                        w = 128 * tiles(o, peeled)
                        wait(pe, relued, i, o)
                        wait(pe, scanned, i, o - 2)
                        pe.matmul(ps_msg[o % 2][:, 0:w], w2[:, :], hid[:, o % 2, 0:w],
                                  start=True, stop=True).then_inc(product[o % RING], 1)
                    if there(off, peeled):
                        nt = tiles(off, peeled)
                        wait(pe, scanned, i, off)
                        wait(pe, turned_copied, i, off - 2)
                        for t in range(nt):
                            mm = pe.transpose(ps_seg[off % 2][:, 128 * t:128 * t + 128],
                                              seg[:, off % RING, t:128 * nt:nt], ident[:, :])
                        mm.then_inc(turned[off % RING], 1)

                chunks(pe, step, ahead=3)

            either(pe, make)

        @block.vector
        def _(dve):
            steps = [0]

            def link(ins):
                steps[0] += 1
                ins.then_inc(dve_step, 1)
                dve.wait_ge(dve_step, steps[0])

            dve.memset(dst_c[:, GF, :], 0).then_inc(dst_zeroed, 1)
            dve.memset(prev_c[:, :], -1).then_inc(dst_zeroed, 1)
            dve.memset(ones_row[:, :], 1.0).then_inc(const_made, 1)
            dve.memset(ones_bf[:, :], 1.0).then_inc(const_made, 1)
            dve.memset(zero1[:, :], 0.0).then_inc(const_made, 1)
            dve.memset(eps[:, :], EPS).then_inc(const_made, 1)
            link(dve.memset(seg[:, RING - 1, CH - 1:CH], 0.0))
            dve.wait_ge(w1_in, 16)
            dve.tensor_copy(w_qp[:, 0, :], w1[:, 1, :]).then_inc(w_made, 1)
            dve.tensor_tensor(w_qp[:, 1, :], w1[:, 0, :], w1[:, 1, :], ALU.subtract).then_inc(w_made, 1)
            dve.wait_ge(b1_in, 16)
            def p_part(i, h):
                    dve.wait_ge(qp_made, 2 * i + h + 1)
                    freed(dve, p_stored[h], 16 * i)
                    dve.tensor_tensor(p_out[:, h, :, :], ps_seg[h][0:NP, 0:2 * D].rearrange("n (k f) -> n k f", k=2),
                                      b1_all[:, :].unsqueeze(1).broadcast_to([NP, 2, D]), ALU.add).then_inc(p_copied, 1)

            turns(dve, KB // 4, p_part)

            dve.wait_ge(dst_in, 48)
            dve.wait_ge(prev_in, 16 * G)
            dve.tensor_copy(prev_f[:, :], prev_c[:, :])
            link(dve.tensor_copy(dst_f[:, :, :], dst_c[:, :, :]))
            dve.tensor_tensor(same[:, :, 1:CH], dst_f[:, :, 1:CH], dst_f[:, :, 0:CH - 1], ALU.is_equal)
            dve.tensor_tensor(same[:, :, 0], dst_f[:, :, 0], prev_f[:, :], ALU.is_equal)
            link(dve.tensor_scalar(base_f[:, :], dst_f[:, :, 0], float(TOP), None, ALU.min))
            dve.tensor_copy(base_i[:, :], base_f[:, :])
            dve.tensor_scalar(row_c[:, :, 0, :], same[:, :, :], -0.5, 2.0 * HALF_BIG, ALU.add, ALU.mult)
            link(dve.tensor_tensor(local[:, :, :], dst_f[:, :, :],
                                   base_f[:, :].unsqueeze(2).broadcast_to([128, G, CH]), ALU.subtract))
            dve.tensor_reduce(far[:, :], local[:, :, :], AX.XY, ALU.max).then_inc(far_made, 1)
            dve.tensor_copy(row_c[:, :, 1, :], local[:, :, :]).then_inc(rows_made, 1)
            dve.wait_ge(far_turned, 1)
            link(dve.tensor_reduce(far1[:, :], ps_hid[0][0:1, 0:128], AX.X, ALU.max))
            dve.tensor_scalar(far_i[:, :], far1[:, :], float(WIN - 1), None, ALU.is_gt).then_inc(flag_made, 1)

            dve.wait_ge(sample_in, 16)
            dve.tensor_copy(sample_f[:, :], sample_i[:, :]).then_inc(sample_cast, 1)
            dve.wait_ge(iota_made, 2)
            dve.tensor_copy(lane[:, :], lane_i[:, :])
            dve.tensor_copy(node[:, :], node_i[:, :])
            dve.wait_ge(sample_spread, 1)
            dve.tensor_copy(sample_all[:, 0:512], ps_msg[0][0:NP, :])
            link(dve.tensor_copy(sample_all[:, 512:SAMPLES], ps_msg[1][0:NP, 0:SAMPLES - 512]))
            def samples_up_to(k):
                freed(dve, coarse_made, k)
                dve.tensor_scalar(junk[:, 0:SAMPLES], sample_all[:, :], node[:, bass.ds(k, 1)], 0.0, ALU.is_le, ALU.add,
                                  accum_out=coarse[:, bass.ds(k, 1)]).then_inc(coarse_made, 1)

            samples_up_to(0)
            with dve.Fori(1, KB) as k:
                samples_up_to(k)
            dve.wait_ge(coarse_made, KB)
            link(dve.tensor_scalar(span_f[:, :], coarse[:, :], -1.0, 0.0, ALU.add, ALU.max))
            def count(i, h):
                dve.wait_ge(span_in[h], 16 * GROUP * (i + 1))
                for k in range(GROUP):
                    freed(dve, fine_made, GROUP * (2 * i + h) + k)
                    at = bass.ds(GROUP * (2 * i + h) + k, 1)
                    low = span_rows[:, h, k, :].bitcast(I16).rearrange("n (j a) -> n j a", a=2)[:, :, 0]
                    dve.tensor_scalar(junk[:, :], low, node[:, at], 0.0, ALU.is_le, ALU.add,
                                      accum_out=fine[:, at]).then_inc(fine_made, 1)

            def name(i, h):
                dve.tensor_copy(span_at[:, h, :], span_f[:, bass.ds(GROUP * (2 * i + h), GROUP)]).then_inc(span_named, 1)

            for h in range(2):
                name(0, h)

            def count_and_name(i, h):
                count(i, h)
                dve.wait_ge(fine_made, GROUP * (2 * i + h + 1))
                name(i + 1, h)

            turns(dve, KB // GROUP // 2 - 1, count_and_name)
            for h in range(2):
                count(KB // GROUP // 2 - 1, h)
            dve.wait_ge(fine_made, KB)
            dve.scalar_tensor_tensor(out=end[:, :], in0=span_f[:, :], scalar=float(SPAN), in1=fine[:, :],
                                     op0=ALU.mult, op1=ALU.add).then_inc(end_made, 1)
            dve.wait_ge(end_made, 1)
            dve.tensor_scalar(last_f[:, :], end[:, :], -1.0, 0.0, ALU.add, ALU.max)
            dve.wait_ge(start_in, 16)
            dve.tensor_tensor(filled[:, :], end[:, :], start[:, :], ALU.is_gt)

            def make(general):
                def step(i, off, peeled):
                    if not general and there(off + 3, peeled):
                        o = off + 3
                        nt = tiles(o, peeled)
                        wait(dve, spread, i, o)
                        wait(dve, summed, i, o - 2)
                        dve.tensor_scalar(pick[:, o % 2, 0:128 * nt].rearrange("n (t p) -> n t p", t=nt),
                                          ps_local[:, 0:128 * nt].rearrange("n (p t) -> n t p", t=nt),
                                          lane[:, 0:1], None, ALU.is_equal).then_inc(picked[o % RING], 1)
                    if there(off + 1, peeled):
                        o = off + 1
                        b, w = o % RING, 128 * tiles(o, peeled)
                        wait(dve, product, i, o)
                        wait(dve, limit_copied, i, o)
                        wait(dve, scanned, i, o - 1)
                        wait(dve, turned, i, o - RING)
                        dve.tensor_tensor_scan(seg[:, b, 0:w], limit[:, b, 0:w], ps_msg[o % 2][:, 0:w],
                                               seg[:, (o - 1) % RING, CH - 1:CH], ALU.min, ALU.max
                                               ).then_inc(scanned[b], 1)

                chunks(dve, step, ahead=3)

            either(dve, make)

            def name_last(i, h):
                dve.tensor_copy(last_at[:, h, :], last_f[:, bass.ds(GROUP * (2 * i + h), GROUP)]).then_inc(last_named, 1)

            def finish(i, h):
                n = 2 * i + h + 1
                dve.wait_ge(top_in[h], 16 * GROUP * (i + 1))
                dve.tensor_tensor(res[:, h, :, :], top[:, h, :, :],
                                  b2_all[:, :].unsqueeze(1).broadcast_to([NP, GROUP, D]), ALU.add).then_inc(top_b2, 1)
                dve.wait_ge(top_b2, n)
                dve.tensor_tensor(top[:, h, :, :], res[:, h, :, :],
                                  filled[:, bass.ds(GROUP * (2 * i + h), GROUP)].unsqueeze(2)
                                  .broadcast_to([NP, GROUP, D]), ALU.mult).then_inc(top_kept, 1)
                dve.wait_ge(top_kept, n)
                dve.wait_ge(x_again[h], 16 * (i + 1))
                dve.tensor_tensor(res[:, h, :, :], top[:, h, :, :], x_r[:, h, :, :], ALU.add).then_inc(res_made, 1)
                dve.wait_ge(res_made, n)
                for k in range(GROUP):
                    dve.bn_stats(stats[:, h, k, :], res[:, h, k, :]).then_inc(stats_made, 1)
                dve.wait_ge(stats_made, GROUP * n)
                apart(dve)
                for k in range(GROUP):
                    ins = dve.bn_aggr(mv[:, h, k, :], stats[:, h, k, :])
                ins.then_inc(mv_made, 1)
                dve.wait_ge(std_made, n)
                dve.reciprocal(rstd[:, h, :, :], std[:, h, :, :]).then_inc(rstd_made, 1)
                dve.wait_ge(rstd_made, n)
                freed(dve, out_stored[h], 16 * i)
                for k in range(GROUP):
                    ins = dve.tensor_scalar(fin[:, h, k, :], res[:, h, k, :], mv[:, h, k, 0:1], rstd[:, h, k, :],
                                            ALU.subtract, ALU.mult)
                ins.then_inc(fin_made, 1)

            dve.wait_ge(b2_in, 16)
            for h in range(2):
                name_last(0, h)

            def finish_and_name(i, h):
                finish(i, h)
                name_last(i + 1, h)

            turns(dve, KB // GROUP // 2 - 1, finish_and_name)
            for h in range(2):
                finish(KB // GROUP // 2 - 1, h)


_INS = ["x", "src", "dst", "L0_gnn_W1", "L0_gnn_b1", "L0_gnn_W2", "L0_gnn_b2"]


def kernel(**inputs):
    import numpy as _np
    import concourse.bacc as _bacc
    from concourse.bass_utils import run_bass_kernel_spmd as _run

    nc = _bacc.Bacc("TRN2", target_bir_lowering=False, num_devices=1)
    arrays, args = {}, []
    for name in _INS:
        a = _np.ascontiguousarray(inputs[name])
        arrays[f"in_{name}_dram"] = a
        args.append(nc.dram_tensor(f"in_{name}_dram", a.shape, mybir.dt.from_np(a.dtype), kind="ExternalInput").ap())
    args.append(nc.dram_tensor("out_0_dram", inputs["x"].shape, F32, kind="ExternalOutput").ap())
    gnn_max_resnorm(nc, *args)
    return _run(nc, [arrays], core_ids=[0]).results[0]["out_0_dram"]
```

```python
from contextlib import ExitStack

import concourse.bass as bass
from concourse import mybir

F32 = mybir.dt.float32
BF16 = mybir.dt.bfloat16
I32 = mybir.dt.int32
U32 = mybir.dt.uint32
I16 = mybir.dt.int16
ALU = mybir.AluOpType
ACT = mybir.ActivationFunctionType
AX = mybir.AxisListType

RING = 4
HALF_BIG = 255.0 * 2.0 ** 119
EPS = 1e-5


def gnn_max_resnorm(nc, x, src, dst, W1, b1, W2, b2, out):
    N, D = x.shape
    E = src.shape[0]

    NP = 125
    KB = N // NP
    assert N == NP * KB and D == 128
    T = 4
    CH = 128 * T
    NC = -(-E // CH)
    LAST = (E - (NC - 1) * CH) // 128
    assert E % 128 == 0 and 1 <= LAST <= T
    FOUR = 4
    AHEAD = 4
    FOURS = KB // FOUR
    GROUP = 5
    assert FOURS % AHEAD == 1 and KB % (2 * GROUP) == 0
    GROUPS = KB // GROUP
    PARTS = 3
    WIN = 128 // PARTS
    TALL = PARTS * WIN
    SPAN = 640
    SAMPLES = E // SPAN
    assert SAMPLES * SPAN == E
    G = -(-NC // 128)
    GF = (NC - 1) // 128
    QF = NC - 1 - 128 * GF

    with ExitStack() as ctx:
        def sb(name, shape, dt=F32):
            return ctx.enter_context(nc.sbuf_tensor(name, shape, dt))

        def ps(name):
            return ctx.enter_context(nc.psum_tensor(name, [128, 512], F32))

        def sem(name):
            return ctx.enter_context(nc.semaphore(name))

        def sems(name, n=RING):
            return [sem(f"{name}{i}") for i in range(n)]

        def dram(name, shape, dt=F32):
            return nc.dram_tensor(name, shape, dt, kind="Internal").ap()

        q_tab = dram("q_tab", [N, D])
        p_tab = dram("p_tab", [N + WIN, PARTS * D], BF16)
        top_tab = dram("top_tab", [N + WIN, D])
        seg_tab = dram("seg_tab", [E, D])
        row_tab = dram("row_tab", [NC, 2 * CH], BF16)
        ends_tab = dram("ends_tab", [NC, CH])
        base_tab = dram("base_tab", [NC, 1], I32)
        flag_tab = dram("flag_tab", [1, 1], I32)
        end_tab = dram("end_tab", [N + 1])

        ident = sb("ident", [128, 128])
        ident_bf = sb("ident_bf", [128, 128], BF16)
        lane_i = sb("lane_i", [128, 1], I32)
        lane = sb("lane", [128, 1])
        place_i = sb("place_i", [128, WIN], I32)
        place = sb("place", [128, WIN])
        thirds = sb("thirds", [128, WIN])
        third = sb("third", [128, 1])
        pad = sb("pad", [WIN, PARTS * D], BF16)
        node_i = sb("node_i", [NP, KB], I32)
        node = sb("node", [NP, KB])
        ones_row = sb("ones_row", [1, 128])
        ones_bf = sb("ones_bf", [1, 128], BF16)
        zero1 = sb("zero1", [1, 1])
        eps = sb("eps", [128, 1])
        w1 = sb("w1", [D, 2, D])
        w_qp = sb("w_qp", [D, 2, D])
        w2 = sb("w2", [D, D])
        b1_col = sb("b1_col", [D, 1])
        b2_all = sb("b2_all", [NP, D])
        x_in = sb("x_in", [NP, AHEAD, FOUR, D])
        x_t = sb("x_t", [D, 2, FOUR, NP])
        qp_out = sb("qp_out", [NP, 2, 2, FOUR, D])
        p_rest = sb("p_rest", [NP, FOUR, D])
        p_parts = sb("p_parts", [NP, 2, FOUR, PARTS, D], BF16)
        room = sb("room", [128, 4, G, CH])
        x_all = room[0:NP].rearrange("n r g j -> n (r g j)")[:, 0:KB * D].rearrange("n (k f) -> n k f", k=KB)
        dst_f, edge_f, dst_c = room[:, 0], room[:, 1], room[:, 2].bitcast(I32)
        prev_c = sb("prev_c", [128, G], I32)
        prev_f = sb("prev_f", [128, G])
        next_c = sb("next_c", [128, G], I32)
        next_f = sb("next_f", [128, G])
        row_c = sb("row_c", [128, G, 2, CH], BF16)
        base_f = sb("base_f", [128, G])
        base_i = sb("base_i", [128, G], I32)
        gap = sb("gap", [128, G])
        wide = sb("wide", [128, 2])
        far = sb("far", [128, 1])
        far1 = sb("far1", [1, 1])
        far_i = sb("far_i", [1, 1], I32)
        sample_i = sb("sample_i", [1, SAMPLES], I32)
        sample_f = sb("sample_f", [1, SAMPLES])
        sample_all = sb("sample_all", [NP, SAMPLES])
        junk = sb("junk", [NP, SPAN], BF16)
        coarse = sb("coarse", [NP, KB])
        span_f = sb("span_f", [NP, KB])
        span_at = sb("span_at", [NP, 2, GROUP], U32)
        span_more = sb("span_more", [NP, GROUP, SPAN], I32)
        span_rows = [row_c[0:NP].rearrange("n g a j -> n (g a j)")[:, 0:2 * GROUP * SPAN].bitcast(I32)
                     .rearrange("n (k j) -> n k j", k=GROUP), span_more]
        fine = sb("fine", [NP, KB])
        end = sb("end", [NP, KB])
        start = sb("start", [NP, KB])
        filled = sb("filled", [NP, KB])
        last_f = sb("last_f", [NP, KB])
        idx = sb("idx", [128, RING, T], I32)
        idx_d = sb("idx_d", [128, RING, T], I32)
        rows = sb("rows", [1, RING, 2, CH], BF16)
        win = sb("win", [TALL, RING, D], BF16)
        q_rows = sb("q_rows", [128, RING, T, D])
        p_rows = sb("p_rows", [128, RING, T, PARTS * D], BF16)
        pick = sb("pick", [TALL, 2, CH], BF16)
        ends = sb("ends", [128, RING, T])
        limit = sb("limit", [128, RING, CH])
        hid = sb("hid", [D, 2, CH])
        seg = sb("seg", [D, RING, CH])
        seg_t = sb("seg_t", [128, 2, T, D + 1])
        chosen = sb("chosen", [128, 2, T, WIN])
        w_top = sb("w_top", [WIN, RING, D])
        last_at = sb("last_at", [NP, 2, GROUP], U32)
        top = sb("top", [NP, 2, GROUP, D])
        res = sb("res", [NP, 2, GROUP, D])
        stats = sb("stats", [NP, 2, GROUP, 6])
        mv = sb("mv", [NP, 2, GROUP, 2])
        std = sb("std", [NP, 2, GROUP, 1])
        rstd = sb("rstd", [NP, 2, GROUP, 1])
        fin = sb("fin", [NP, 2, GROUP, D])

        ps_local = ps("ps_local")
        ps_limit = ps("ps_limit")
        ps_hid = [ps("ps_hid0"), ps("ps_hid1")]
        ps_msg = [ps("ps_msg0"), ps("ps_msg1")]
        ps_seg = ps("ps_seg")
        ps_top = ps("ps_top")

        ident_zeroed, ident_made, iota_made, const_made = (sem("ident_zeroed"), sem("ident_made"),
                                                           sem("iota_made"), sem("const_made"))
        w1_in, w2_in, b1_in, b2_in, w_made = sem("w1_in"), sem("w2_in"), sem("b1_in"), sem("b2_in"), sem("w_made")
        ones_col_made = sem("ones_col_made")
        x_loaded = sems("x_loaded", AHEAD)
        xt_made, xt_copied, qp_made = sem("xt_made"), sem("xt_copied"), sem("qp_made")
        qp_copied, q_stored, p_stored = sem("qp_copied"), sems("q_stored", 2), sems("p_stored", 2)
        part_made, pad_made, pad_stored, ident_bf_made = (sem("part_made"), sem("pad_made"), sem("pad_stored"),
                                                          sem("ident_bf_made"))
        dst_filled, dst_in, near_in, sample_in = sem("dst_filled"), sem("dst_in"), sem("near_in"), sem("sample_in")
        dve_step = sem("dve_step")
        rows_made, rows_stored, ends_stored = sem("rows_made"), sem("rows_stored"), sem("ends_stored")
        last_marked, dst_cast, local_made, same_made = (sem("last_marked"), sem("dst_cast"), sem("local_made"),
                                                        sem("same_made"))
        base_made, base_stored = sem("base_made"), sem("base_stored")
        far_made, far_turned, flag_made, flag_stored = (sem("far_made"), sem("far_turned"), sem("flag_made"),
                                                        sem("flag_stored"))
        node_cast = sem("node_cast")
        sample_cast, sample_spread, coarse_made = sem("sample_cast"), sem("sample_spread"), sem("coarse_made")
        span_named, span_in, fine_made = sem("span_named"), sems("span_in", 2), sem("fine_made")
        zero_stored, end_made, end_stored, start_in = (sem("zero_stored"), sem("end_made"), sem("end_stored"),
                                                       sem("start_in"))

        idx_in, rows_in, win_in, gathered = sems("idx_in"), sems("rows_in"), sems("win_in"), sems("gathered")
        spread, picked, limit_copied = sem("spread"), sem("picked"), sem("limit_copied")
        summed, relued, product, scanned = sem("summed"), sem("relued"), sem("product"), sem("scanned")
        turned, turned_copied, seg_stored = sem("turned"), sem("turned_copied"), sems("seg_stored")
        ends_in, chosen_made, topped = sems("ends_in"), sem("chosen_made"), sem("topped")
        w_top_made = sem("w_top_made")
        w_stored = sems("w_stored")

        last_named, top_in, x_again = sem("last_named"), sems("top_in", 2), sem("x_again")
        top_b2, top_kept, res_made, stats_made, mv_made = (sem("top_b2"), sem("top_kept"), sem("res_made"),
                                                           sem("stats_made"), sem("mv_made"))
        std_made, rstd_made, fin_made, out_stored = (sem("std_made"), sem("rstd_made"), sem("fin_made"),
                                                     sems("out_stored", 2))

        ctx.enter_context(nc.allow_non_contiguous_dma(reason="one dst for each chunk or span"))
        passed = sem("passed")

        block = ctx.enter_context(nc.Block())

        def wait(eng, stage, i, off, by=1):
            if isinstance(stage, list):
                stage, value = stage[off % RING], (i + off // RING + 1) * by
            else:
                value = RING * i + off + 1
            freed(eng, stage, value)

        def tiles(off, peeled):
            return LAST if peeled and off == NC - 1 else T

        def chunks(eng, step, ahead=0, behind=0, rings=1):
            turn = rings * RING
            loops = (NC - RING) // turn
            for s in range(-ahead, turn):
                step(0, s, True)
            with eng.Fori(1, loops) as i:
                for off in range(turn):
                    step(i if rings == 1 else i * rings, off, False)
            for s in range(loops * turn, NC + behind):
                step(0, s, True)

        def turns(eng, n, body):
            for h in range(2):
                body(0, h)
            with eng.Fori(1, n) as i:
                for h in range(2):
                    body(i, h)

        def freed(eng, semaphore, value):
            if not isinstance(value, int) or value > 0:
                eng.wait_ge(semaphore, value)

        def fours(eng, body):
            for h in range(AHEAD):
                body(0, h)
            with eng.Fori(1, FOURS // AHEAD) as i:
                for h in range(AHEAD):
                    body(i, h)
            body(FOURS // AHEAD, 0)

        def groups(eng, step):
            for h in range(2):
                step(0, h)
            with eng.Fori(1, GROUPS // 2 - 2) as i:
                for h in range(2):
                    step(i, h)
            for n in range(GROUPS - 4, GROUPS):
                step(n // 2, n % 2)

        def is_group(i, h, ahead=0):
            return not isinstance(i, int) or 2 * i + h + ahead < GROUPS

        def there(off, peeled):
            return not peeled or 0 <= off < NC

        def either(eng, windows, general):
            eng.wait_ge(flag_stored, 16)
            flag = eng.value_load(flag_tab[0:1, 0:1], min_val=0, max_val=1)
            with eng.If(flag == 0):
                windows()
            with eng.Else():
                general()

        def apart(eng):
            eng.sem_inc(passed, 1)

        def chunk_rows(table, tile):
            return ((table[0:GF * 128].rearrange("(g q) j -> q g j", q=128), tile[:, 0:GF, :]),
                    (table[GF * 128:NC], tile[0:QF + 1, GF, :]))

        def blocks_of(table):
            return table.rearrange("(p k) f -> p k f", k=KB)

        @block.sync
        def _(sp):
            def load_x(i, h):
                freed(sp, xt_made, AHEAD * (i - 1) + h + 1)
                sp.dma_start(x_in[:, h, :, :],
                             blocks_of(x)[:, bass.ds(FOUR * (AHEAD * i + h), FOUR), :]).then_inc(x_loaded[h], 16)

            def store_qp(i, h):
                n, slot = AHEAD * i + h, h % 2
                at = bass.ds(FOUR * n, FOUR)
                sp.wait_ge(qp_copied, 2 * (n + 1))
                sp.dma_start(blocks_of(q_tab)[:, at, :], qp_out[:, slot, 0, :, :]).then_inc(q_stored[slot], 16)
                sp.wait_ge(part_made, PARTS * (n + 1))
                sp.dma_start(blocks_of(p_tab[0:N])[:, at, :],
                             p_parts[:, slot, :, :, :].rearrange("n k a f -> n k (a f)")).then_inc(p_stored[slot], 16)

            load_x(0, 0)
            sp.dma_start(w1[:, :, :], W1.rearrange("(a f) o -> f a o", a=2)).then_inc(w1_in, 16)
            for h in range(1, AHEAD):
                load_x(0, h)
            sp.wait_ge(dst_filled, 3)
            sp.dma_start(dst_c[:, 0:GF, :],
                         dst[0:GF * 128 * CH].rearrange("(g q j) -> q g j", q=128, j=CH)).then_inc(dst_in, 16)
            sp.dma_start(dst_c[0:QF, GF, :],
                         dst[GF * 128 * CH:(NC - 1) * CH].rearrange("(q j) -> q j", j=CH)).then_inc(dst_in, 16)
            sp.dma_start(dst_c[QF:QF + 1, GF, 0:LAST * 128],
                         dst[(NC - 1) * CH:E].rearrange("(q j) -> q j", q=1)).then_inc(dst_in, 16)
            each = dst.rearrange("(e a) -> e a", a=1)
            for g in range(G):
                lo, n = (1 if g == 0 else 0), (128 if g < GF else QF + 1)
                first = (128 * g + lo) * CH - 1
                sp.dma_start(prev_c[lo:n, g:g + 1],
                             each[first:first + (n - lo - 1) * CH + 1:CH, :]).then_inc(near_in, 16)
                n = 128 if g < GF else QF
                first = (128 * g + 1) * CH
                sp.dma_start(next_c[0:n, g:g + 1],
                             each[first:first + (n - 1) * CH + 1:CH, :]).then_inc(near_in, 16)
            sp.dma_start(w2[:, :], W2).then_inc(w2_in, 16)
            sp.dma_start(b1_col[:, :], b1.rearrange("(f a) -> f a", a=1)).then_inc(b1_in, 16)
            sp.dma_start(b2_all[:, :], b2.partition_broadcast(NP)).then_inc(b2_in, 16)

            def load_idx(i, off, peeled):
                b, nt = off % RING, tiles(off, peeled)
                wait(sp, gathered, i, off - RING, 16 * T)
                sp.dma_start(idx[:, b, 0:nt], src[bass.ds(CH * RING * i + CH * off, 128 * nt)]
                             .rearrange("(p t) -> p t", t=nt)).then_inc(idx_in[b], 16)

            for c in range(RING):
                load_idx(0, c, True)

            def products(i, h):
                if h == 0 or not isinstance(i, int) or i + 1 < FOURS // AHEAD:
                    load_x(i + 1, h)
                store_qp(i, h)

            for h in range(AHEAD):
                products(0, h)
            with sp.Fori(1, FOURS // AHEAD - 1) as i:
                for h in range(AHEAD):
                    products(i, h)
            for h in range(AHEAD):
                products(FOURS // AHEAD - 1, h)
            store_qp(FOURS // AHEAD, 0)
            sp.wait_ge(pad_made, 1)
            sp.dma_start(p_tab[N:N + WIN, :], pad[:, :]).then_inc(pad_stored, 16)
            sp.wait_ge(flag_made, 1)
            sp.dma_start(flag_tab[:, :], far_i[:, :]).then_inc(flag_stored, 16)
            sp.wait_ge(base_made, 1)
            for to, of in chunk_rows(base_tab, base_i[:, :].unsqueeze(2)):
                sp.dma_start(to, of).then_inc(base_stored, 16)
            sp.wait_ge(rows_made, 1)
            for to, of in chunk_rows(row_tab, row_c[:, :, :, :].rearrange("q g n j -> q g (n j)")):
                sp.dma_start(to, of).then_inc(rows_stored, 16)
            sp.wait_ge(rows_made, 2)
            for to, of in chunk_rows(ends_tab, edge_f):
                sp.dma_start(to, of).then_inc(ends_stored, 16)
            sp.wait_ge(rows_stored, 32)
            sp.wait_ge(base_stored, 32)
            sp.wait_ge(pad_stored, 16)
            sp.wait_ge(p_stored[0], 16 * (FOURS // 2 + 1))
            sp.wait_ge(p_stored[1], 16 * (FOURS // 2))

            def load_part_of_x(part):
                at = slice(2 * GROUP * part, 2 * GROUP * (part + 1))
                sp.dma_start(x_all[:, at, :], blocks_of(x)[:, at, :]).then_inc(x_again, 16)

            def store_out(i, h):
                sp.wait_ge(fin_made, 2 * i + h + 1)
                sp.dma_start(blocks_of(out)[:, bass.ds(GROUP * (2 * i + h), GROUP), :],
                             fin[:, h, :, :]).then_inc(out_stored[h], 16)

            def load(i, off, peeled, general):
                b, nt = off % RING, tiles(off, peeled)
                if general:
                    wait(sp, gathered, i, off - RING, 2 * 16 * T)
                    sp.dma_start(idx_d[:, b, 0:nt], dst[bass.ds(CH * RING * i + CH * off, 128 * nt)]
                                 .rearrange("(p t) -> p t", t=nt)).then_inc(idx_in[b], 16)
                if not peeled or off >= RING:
                    load_idx(i, off, peeled)
                wait(sp, spread, i, off - RING)
                sp.dma_start(rows[:, b, :, :], row_tab[bass.ds(RING * i + off, 1), :]
                             .rearrange("a (n j) -> a n j", n=2)).then_inc(rows_in[b], 16)

            def windows():
                def step(i, off, peeled):
                    if there(off + RING, peeled):
                        load(i, off + RING, peeled, False)
                        o = off + RING
                        b = o % RING
                        first = sp.value_load(base_tab[bass.ds(RING * i + o, 1), 0:1], min_val=0, max_val=N - 1)
                        wait(sp, summed, i, o - RING)
                        sp.dma_start(win[:, b, :], p_tab[bass.ds(first, WIN), :]
                                     .rearrange("n (a f) -> (n a) f", a=PARTS)).then_inc(win_in[b], 16)
                    if peeled and off == -2:
                        sp.wait_ge(ends_stored, 32)
                    if there(off + 2, peeled):
                        o = off + 2
                        b, nt = o % RING, tiles(o, peeled)
                        wait(sp, chosen_made, i, o - RING)
                        sp.dma_start(ends[:, b, 0:nt],
                                     ends_tab[bass.ds(RING * i + o, 1), 0:128 * nt]
                                     .rearrange("a (p t) -> (a p) t", t=nt)).then_inc(ends_in[b], 16)
                    if peeled and 0 <= off < GROUPS // 2:
                        load_part_of_x(off)

                chunks(sp, step, ahead=RING, rings=4)
                for c in range(NC - RING, NC):
                    wait(sp, w_stored, 0, c, 16)

                def load_top(i, h):
                    freed(sp, res_made, 2 * i + h - 1)
                    sp.dma_start(top[:, h, :, :], blocks_of(top_tab[0:N])[:, bass.ds(GROUP * (2 * i + h), GROUP), :]
                                 ).then_inc(top_in[h], 16)

                for h in range(2):
                    load_top(0, h)

                def finish(i, h):
                    if is_group(i, h, 2):
                        load_top(i + 1, h)
                    store_out(i, h)

                groups(sp, finish)

            def general():
                def step(i, off, peeled):
                    if there(off + RING, peeled):
                        load(i, off + RING, peeled, True)
                    if there(off, peeled):
                        b, nt = off % RING, tiles(off, peeled)
                        wait(sp, turned_copied, i, off)
                        sp.dma_start(seg_tab[bass.ds(CH * RING * i + CH * off, 128 * nt), :]
                                     .rearrange("(p t) f -> p t f", t=nt),
                                     seg_t[:, off % 2, 0:nt, 0:D]).then_inc(seg_stored[b], 16)

                sp.wait_ge(ends_stored, 32)
                for part in range(GROUPS // 2):
                    load_part_of_x(part)
                chunks(sp, step, ahead=RING)
                sp.dma_start(sample_i[:, :],
                             dst.rearrange("(a s j) -> a s j", a=1, j=SPAN)[:, :, 0]).then_inc(sample_in, 16)
                sp.dma_start(end_tab[0:1].rearrange("(a b) -> a b", a=1), zero1[:, :]).then_inc(zero_stored, 16)
                sp.wait_ge(end_made, 1)
                sp.dma_start(end_tab[1:N + 1].rearrange("(p k) -> p k", k=KB), end[:, :]).then_inc(end_stored, 16)
                sp.wait_ge(end_stored, 16)
                sp.wait_ge(zero_stored, 16)
                sp.dma_start(start[:, :], end_tab[0:N].rearrange("(p k) -> p k", k=KB)).then_inc(start_in, 16)

                groups(sp, store_out)

            either(sp, windows, general)
            for h in range(2):
                sp.wait_ge(out_stored[h], 16 * (GROUPS // 2))

        @block.gpsimd
        def _(pool):
            pool.memset(dst_c[:, GF, :], -1).then_inc(dst_filled, 1)
            pool.memset(prev_c[:, :], -1).then_inc(dst_filled, 1)
            pool.memset(next_c[:, :], -1).then_inc(last_marked, 1)
            pool.wait_ge(last_marked, 1)
            pool.affine_select(out=next_c[:, GF:G], in_=next_c[:, GF:G], compare_op=ALU.not_equal, fill=N,
                               base=-QF, pattern=[[0, 1]], channel_multiplier=1).then_inc(dst_filled, 1)
            pool.memset(ident[:, :], 0.0).then_inc(ident_zeroed, 1)
            pool.wait_ge(ident_zeroed, 1)
            pool.affine_select(out=ident[:, :], in_=ident[:, :], compare_op=ALU.not_equal, fill=1.0, base=0,
                               pattern=[[-1, 128]], channel_multiplier=1).then_inc(ident_made, 1)
            pool.iota(lane_i[:, :], pattern=[[0, 1]], base=0, channel_multiplier=1).then_inc(iota_made, 1)
            pool.iota(place_i[:, :], pattern=[[1, WIN]], base=1, channel_multiplier=0).then_inc(iota_made, 1)
            pool.iota(node_i[:, :], pattern=[[1, KB]], base=0, channel_multiplier=KB).then_inc(iota_made, 1)

            pool.memset(pad[:, :], 0.0).then_inc(pad_made, 1)
            pool.wait_ge(dst_cast, 1)
            pool.tensor_tensor(row_c[:, :, 1, :], dst_f[:, :, :],
                               base_f[:, :].unsqueeze(2).broadcast_to([128, G, CH]), ALU.subtract).then_inc(local_made, 1)
            pool.wait_ge(ident_made, 1)
            pool.tensor_copy(ident_bf[:, :], ident[:, :]).then_inc(ident_bf_made, 1)

            pool.wait_ge(q_stored[0], 16 * (FOURS // 2 + 1))
            pool.wait_ge(q_stored[1], 16 * (FOURS // 2))

            def gather(i, off, peeled, rows_of, table, at):
                b = off % RING
                for t in range(tiles(off, peeled)):
                    pool.indirect_dma_start(
                        out=rows_of[:, b, t, :], out_offset=None, in_=table,
                        in_offset=bass.IndirectOffsetOnAxis(ap=at[:, b, t:t + 1].bitcast(U32), axis=0)
                    ).then_inc(gathered[b], 16)

            for c in range(RING):
                wait(pool, idx_in, 0, c, 16)
                gather(0, c, True, q_rows, q_tab, idx)

            def gathers(general):
                def step(i, off, peeled):
                    early = peeled and off < RING
                    if general or not early:
                        wait(pool, idx_in, i, off, 32 if general else 16)
                        wait(pool, summed, i, off - RING)
                        apart(pool)
                    if not early:
                        gather(i, off, peeled, q_rows, q_tab, idx)
                    if general:
                        gather(i, off, peeled, p_rows, p_tab[0:N], idx_d)

                chunks(pool, step, rings=4)

            def general():
                pool.wait_ge(p_stored[0], 16 * (FOURS // 2 + 1))
                pool.wait_ge(p_stored[1], 16 * (FOURS // 2))
                gathers(True)
                spans = dst.rearrange("(s j) -> s j", j=SPAN)

                def fetch_spans(i, h):
                    pool.wait_ge(span_named, 2 * i + h + 1)
                    apart(pool)
                    for k in range(GROUP):
                        pool.indirect_dma_start(
                            out=span_rows[h][:, k, :], out_offset=None, in_=spans,
                            in_offset=bass.IndirectOffsetOnAxis(ap=span_at[:, h, k:k + 1], axis=0)
                        ).then_inc(span_in[h], 16)

                turns(pool, KB // GROUP // 2, fetch_spans)
                for c in range(NC - RING, NC):
                    wait(pool, seg_stored, 0, c, 16)

                def fetch_tops(i, h):
                    pool.wait_ge(last_named, 2 * i + h + 1)
                    apart(pool)
                    for k in range(GROUP):
                        pool.indirect_dma_start(
                            out=top[:, h, k, :], out_offset=None, in_=seg_tab,
                            in_offset=bass.IndirectOffsetOnAxis(ap=last_at[:, h, k:k + 1], axis=0)
                        ).then_inc(top_in[h], 16)

                turns(pool, KB // GROUP // 2, fetch_tops)

            either(pool, lambda: gathers(False), general)

        @block.scalar
        def _(act):
            def copy_turned(i, h):
                n, slot = AHEAD * i + h, h % 2
                act.wait_ge(xt_made, n + 1)
                freed(act, qp_made, 2 * (n - 1))
                act.activation(x_t[:, slot, :, :], ps_hid[slot][:, 0:FOUR * NP].rearrange("f (k n) -> f k n", k=FOUR),
                               ACT.Copy).then_inc(xt_copied, 1)

            def tables(i, h):
                n, slot = AHEAD * i + h, h % 2
                if h + 1 < AHEAD and (not isinstance(i, int) or i < FOURS // AHEAD):
                    copy_turned(i, h + 1)
                elif h + 1 == AHEAD:
                    copy_turned(i + 1, 0)
                freed(act, q_stored[slot], 16 * (2 * i + h // 2))
                freed(act, p_stored[slot], 16 * (2 * i + h // 2))
                freed(act, part_made, PARTS * (n - 1))
                for half in range(2):
                    blocks = slice(2 * half, 2 * half + 2)
                    from_ps = ps_msg[half][0:NP, :].rearrange("n (k a f) -> n k a f", k=2, a=2)
                    act.wait_ge(qp_made, 2 * n + half + 1)
                    act.activation(qp_out[:, slot, :, blocks, :].rearrange("n a k f -> n k a f"), from_ps, ACT.Copy)
                    act.activation(p_parts[:, slot, blocks, 0, :], from_ps[:, :, 1, :], ACT.Copy).then_inc(qp_copied, 1)

            copy_turned(0, 0)
            fours(act, tables)
            act.wait_ge(b1_in, 16)

            def bounds(i, o):
                wait(act, spread, i, o)
                wait(act, scanned, i, o - RING)
                act.activation(limit[:, o % RING, :], ps_limit[:, :], ACT.Copy,
                               scale=2.0).then_inc(limit_copied, 1)

            def hidden(i, o, nt):
                wait(act, summed, i, o)
                wait(act, product, i, o - 2)
                act.activation(hid[:, o % 2, 0:128 * nt].rearrange("f (p t) -> f p t", t=nt),
                               ps_hid[o % 2][:, 0:128 * nt].rearrange("f (t p) -> f p t", t=nt),
                               ACT.Relu, bias=b1_col[:, 0:1]).then_inc(relued, 1)

            def turned_rows(i, o, nt):
                wait(act, turned, i, o)
                act.activation(seg_t[:, o % 2, 0:nt, 0:D],
                               ps_seg[:, 0:128 * nt].rearrange("p (t f) -> p t f", t=nt),
                               ACT.Copy).then_inc(turned_copied, 1)

            def windows():
                def step(i, off, peeled):
                    if there(off + 3, peeled):
                        bounds(i, off + 3)
                    if there(off + 2, peeled):
                        hidden(i, off + 2, tiles(off + 2, peeled))
                    if there(off, peeled):
                        wait(act, topped, i, off - 2)
                        turned_rows(i, off, tiles(off, peeled))
                    if there(off - 3, peeled):
                        o = off - 3
                        first = act.value_load(base_tab[bass.ds(RING * i + o, 1), 0:1], min_val=0, max_val=N - 1)
                        wait(act, w_top_made, i, o)
                        wait(act, w_stored, i, o - 1, 16)
                        act.dma_start(top_tab[bass.ds(first, WIN), :], w_top[:, o % RING, :]).then_inc(w_stored[o % RING], 16)

                chunks(act, step, ahead=3, behind=3)

            def general():
                def step(i, off, peeled):
                    if there(off + 3, peeled):
                        bounds(i, off + 3)
                    if there(off + 2, peeled):
                        hidden(i, off + 2, tiles(off + 2, peeled))
                    if there(off, peeled):
                        wait(act, seg_stored, i, off - 2, 16)
                        turned_rows(i, off, tiles(off, peeled))

                chunks(act, step, ahead=3)

            either(act, windows, general)

            def deviations(i, h):
                act.wait_ge(mv_made, 2 * i + h + 1)
                act.activation(std[:, h, :, :], mv[:, h, :, 1:2], ACT.Sqrt, bias=eps[0:NP, 0:1]).then_inc(std_made, 1)

            turns(act, GROUPS // 2, deviations)

        @block.tensor
        def _(pe):
            pe.wait_ge(ident_made, 1)

            def turn_x(i, h):
                pe.wait_ge(x_loaded[h], 16 * i + 16)
                freed(pe, xt_copied, AHEAD * i + h - 1)
                for k in range(FOUR):
                    mm = pe.transpose(ps_hid[h % 2][:, NP * k:NP * k + NP], x_in[:, h, k, :], ident[0:NP, 0:NP])
                mm.then_inc(xt_made, 1)

            def products(i, h):
                pe.wait_ge(xt_copied, AHEAD * i + h + 1)
                for half in range(2):
                    freed(pe, qp_copied, 2 * (AHEAD * i + h) + half - 1)
                    for k in range(2):
                        mm = pe.matmul(ps_msg[half][0:NP, 2 * D * k:2 * D * k + 2 * D], x_t[:, h % 2, 2 * half + k, :],
                                       w_qp[:, :, :].rearrange("f a o -> f (a o)"), start=True, stop=True)
                    mm.then_inc(qp_made, 1)

            turn_x(0, 0)
            pe.wait_ge(w_made, 2)

            def tables(i, h):
                turn_x(*((i, h + 1) if h + 1 < AHEAD else (i + 1, 0)))
                products(i, h)

            for h in range(AHEAD):
                tables(0, h)
            with pe.Fori(1, FOURS // AHEAD) as i:
                for h in range(AHEAD):
                    tables(i, h)
            products(FOURS // AHEAD, 0)

            pe.wait_ge(far_made, 1)
            pe.transpose(ps_top[0:1, 0:128], far[:, 0:1], ident[:, :]).then_inc(far_turned, 1)
            pe.wait_ge(w2_in, 16)
            pe.wait_ge(const_made, 4)
            pe.wait_ge(flag_made, 1)
            pe.wait_ge(qp_copied, 2 * FOURS)
            pe.wait_ge(flag_made, 1)

            def spread_rows(i, o, general):
                wait(pe, rows_in, i, o, 16)
                if not general:
                    wait(pe, picked, i, o - 1)
                    pe.matmul(ps_local[0:TALL, :], ones_bf[0:1, 0:TALL], rows[0:1, o % RING, 1, :], start=True, stop=True)
                wait(pe, limit_copied, i, o - 1)
                pe.matmul(ps_limit[:, :], ones_bf[0:1, :], rows[0:1, o % RING, 0, :],
                          start=True, stop=True).then_inc(spread, 1)

            def sum_up(i, o, peeled, general):
                b, nt = o % RING, tiles(o, peeled)
                wait(pe, relued, i, o - 2)
                if peeled and nt < T:
                    pe.wait_ge(gathered[b], 16 * (2 if general else 1) * (T * (o // RING) + nt))
                else:
                    wait(pe, gathered, i, o, 16 * T * (2 if general else 1))
                for t in range(nt):
                    pe.matmul(ps_hid[o % 2][:, 128 * t:128 * t + 128], q_rows[:, b, t, :], ident[:, :],
                              start=(t == 0), stop=False, is_transpose=True, skip_group_check=True)
                if general:
                    for t in range(nt):
                        for a in range(PARTS):
                            mm = pe.matmul(ps_hid[o % 2][:, 128 * t:128 * t + 128], p_rows[:, b, t, D * a:D * a + D],
                                           ident_bf[:, :], start=False, stop=(t == nt - 1 and a == PARTS - 1),
                                           skip_group_check=True)
                else:
                    wait(pe, win_in, i, o, 16)
                    wait(pe, picked, i, o)
                    mm = pe.matmul(ps_hid[o % 2][:, 0:128 * nt], win[:, b, :], pick[:, o % 2, 0:128 * nt],
                                   start=False, stop=True, skip_group_check=True)
                mm.then_inc(summed, 1)

            def message(i, o, nt):
                wait(pe, relued, i, o)
                wait(pe, scanned, i, o - 2)
                pe.matmul(ps_msg[o % 2][:, 0:128 * nt], w2[:, :], hid[:, o % 2, 0:128 * nt],
                          start=True, stop=True).then_inc(product, 1)

            def turn(i, o, nt):
                wait(pe, scanned, i, o)
                wait(pe, turned_copied, i, o - 1)
                for t in range(nt):
                    mm = pe.transpose(ps_seg[:, 128 * t:128 * t + 128], seg[:, o % RING, t:128 * nt:nt], ident[:, :])
                mm.then_inc(turned, 1)

            def windows():
                def step(i, off, peeled):
                    if there(off + 3, peeled):
                        spread_rows(i, off + 3, False)
                    if there(off + 2, peeled):
                        sum_up(i, off + 2, peeled, False)
                    if there(off + 1, peeled):
                        message(i, off + 1, tiles(off + 1, peeled))
                    if there(off, peeled):
                        turn(i, off, tiles(off, peeled))
                    if there(off - 1, peeled):
                        o = off - 1
                        nt = tiles(o, peeled)
                        wait(pe, turned_copied, i, o)
                        wait(pe, chosen_made, i, o)
                        wait(pe, w_top_made, i, o - 1)
                        for t in range(nt):
                            mm = pe.matmul(ps_top[0:WIN, 0:D + 1], chosen[:, o % 2, t, :], seg_t[:, o % 2, t, :],
                                           start=(t == 0), stop=(t == nt - 1))
                        mm.then_inc(topped, 1)

                pe.wait_ge(ones_col_made, 1)
                chunks(pe, step, ahead=3, behind=1)

            def general():
                pe.wait_ge(ident_bf_made, 1)

                def step(i, off, peeled):
                    if there(off + 3, peeled):
                        spread_rows(i, off + 3, True)
                    if there(off + 2, peeled):
                        sum_up(i, off + 2, peeled, True)
                    if there(off + 1, peeled):
                        message(i, off + 1, tiles(off + 1, peeled))
                    if there(off, peeled):
                        turn(i, off, tiles(off, peeled))

                chunks(pe, step, ahead=3)
                pe.wait_ge(sample_cast, 1)
                for h, (lo, n) in enumerate(((0, 512), (512, SAMPLES - 512))):
                    mm = pe.matmul(ps_msg[h][0:NP, 0:n], ones_row[0:1, 0:NP], sample_f[0:1, lo:lo + n],
                                   start=True, stop=True)
                mm.then_inc(sample_spread, 1)

            either(pe, windows, general)

        @block.vector
        def _(dve):
            steps = [0]

            def link(ins):
                steps[0] += 1
                ins.then_inc(dve_step, 1)
                dve.wait_ge(dve_step, steps[0])

            dve.wait_ge(w1_in, 16)
            dve.tensor_copy(w_qp[:, 0, :], w1[:, 1, :]).then_inc(w_made, 1)
            dve.tensor_tensor(w_qp[:, 1, :], w1[:, 0, :], w1[:, 1, :], ALU.subtract).then_inc(w_made, 1)
            dve.memset(ones_row[:, :], 1.0).then_inc(const_made, 1)
            dve.memset(ones_bf[:, :], 1.0).then_inc(const_made, 1)
            dve.memset(zero1[:, :], 0.0).then_inc(const_made, 1)
            dve.memset(eps[:, :], EPS).then_inc(const_made, 1)
            dve.memset(seg[:, RING - 1, CH - 1:CH], 0.0)
            dve.memset(seg_t[:, :, :, D:D + 1], 1.0).then_inc(ones_col_made, 1)
            dve.wait_ge(iota_made, 3)
            dve.tensor_copy(lane[:, :], lane_i[:, :])
            link(dve.tensor_copy(place[:, :], place_i[:, :]))
            link(dve.tensor_scalar(thirds[:, :], place[:, :], float(PARTS), lane[:, 0:1], ALU.mult, ALU.is_le))
            dve.tensor_reduce(third[:, :], thirds[:, :], AX.X, ALU.add)

            dve.wait_ge(dst_in, 48)
            dve.wait_ge(near_in, 32 * G)
            dve.tensor_copy(next_f[:, :], next_c[:, :])
            dve.tensor_copy(prev_f[:, :], prev_c[:, :])
            link(dve.tensor_copy(dst_f[:, :, :], dst_c[:, :, :]))
            link(dve.tensor_copy(base_f[:, :], dst_f[:, :, 0]))
            link(dve.memset(base_f[0:1, 0:1], 0.0))
            dve.tensor_copy(base_i[:, :], base_f[:, :]).then_inc(base_made, 1)
            dve.sem_inc(dst_cast, 1)
            dve.tensor_tensor(edge_f[:, :, 1:CH], dst_f[:, :, 1:CH], dst_f[:, :, 0:CH - 1], ALU.is_equal)
            dve.tensor_tensor(edge_f[:, :, 0], dst_f[:, :, 0], prev_f[:, :], ALU.is_equal).then_inc(same_made, 1)

            def split(i, h):
                n, slot = AHEAD * i + h, h % 2
                dve.wait_ge(qp_copied, 2 * n + 2)
                freed(dve, part_made, PARTS * n)
                dve.tensor_tensor(p_rest[:, :, :], qp_out[:, slot, 1, :, :], p_parts[:, slot, :, 0, :],
                                  ALU.subtract).then_inc(part_made, 1)
                dve.wait_ge(part_made, PARTS * n + 1)
                dve.tensor_copy(p_parts[:, slot, :, 1, :], p_rest[:, :, :]).then_inc(part_made, 1)
                dve.wait_ge(part_made, PARTS * n + 2)
                dve.tensor_tensor(p_parts[:, slot, :, 2, :], p_rest[:, :, :], p_parts[:, slot, :, 1, :],
                                  ALU.subtract).then_inc(part_made, 1)

            fours(dve, split)
            dve.wait_ge(local_made, 1)
            link(dve.tensor_tensor(gap[:, :], next_f[:, :], base_f[:, :], ALU.subtract))
            dve.tensor_reduce(wide[:, 0:1], row_c[:, :, 1, :], AX.XY, ALU.max)
            link(dve.tensor_reduce(wide[:, 1:2], gap[:, :], AX.X, ALU.max))
            dve.scalar_tensor_tensor(out=far[:, :], in0=wide[:, 1:2], scalar=-1.0, in1=wide[:, 0:1],
                                     op0=ALU.add, op1=ALU.max).then_inc(far_made, 1)
            dve.wait_ge(same_made, 1)
            dve.tensor_scalar(row_c[:, :, 0, :], edge_f[:, :, :], -0.5, 2.0 * HALF_BIG,
                              ALU.add, ALU.mult).then_inc(rows_made, 1)
            dve.wait_ge(far_turned, 1)
            link(dve.tensor_reduce(far1[:, :], ps_top[0:1, 0:128], AX.X, ALU.max))
            dve.tensor_scalar(far_i[:, :], far1[:, :], float(WIN - 1), None, ALU.is_gt).then_inc(flag_made, 1)
            dve.wait_ge(rows_made, 1)
            dve.tensor_tensor(edge_f[:, :, 0:CH - 1], dst_f[:, :, 0:CH - 1], dst_f[:, :, 1:CH], ALU.not_equal)
            link(dve.tensor_tensor(edge_f[:, :, CH - 1], dst_f[:, :, CH - 1], next_f[:, :], ALU.not_equal))
            dve.scalar_tensor_tensor(out=edge_f[:, :, :], in0=row_c[:, :, 1, :], scalar=1.0, in1=edge_f[:, :, :],
                                     op0=ALU.add, op1=ALU.mult).then_inc(rows_made, 1)
            dve.wait_ge(b2_in, 16)

            def center(i, h):
                n = 2 * i + h
                dve.wait_ge(top_in[h], 16 * (i + 1))
                freed(dve, fin_made, n - 1)
                dve.tensor_tensor(res[:, h, :, :], top[:, h, :, :], x_all[:, bass.ds(GROUP * n, GROUP), :],
                                  ALU.add).then_inc(res_made, 1)
                dve.wait_ge(res_made, n + 1)
                for k in range(GROUP):
                    dve.bn_stats(stats[:, h, k, :], res[:, h, k, :]).then_inc(stats_made, 1)
                dve.wait_ge(stats_made, GROUP * (n + 1))
                apart(dve)
                for k in range(GROUP):
                    ins = dve.bn_aggr(mv[:, h, k, :], stats[:, h, k, :])
                ins.then_inc(mv_made, 1)

            def scale(i, h):
                n = 2 * i + h
                dve.wait_ge(std_made, n + 1)
                dve.reciprocal(rstd[:, h, :, :], std[:, h, :, :]).then_inc(rstd_made, 1)
                dve.wait_ge(rstd_made, n + 1)
                freed(dve, out_stored[h], 16 * i)
                for k in range(GROUP):
                    ins = dve.tensor_scalar(fin[:, h, k, :], res[:, h, k, :], mv[:, h, k, 0:1], rstd[:, h, k, :],
                                            ALU.subtract, ALU.mult)
                ins.then_inc(fin_made, 1)

            def scan(i, o, nt):
                b, w = o % RING, 128 * nt
                wait(dve, product, i, o)
                wait(dve, limit_copied, i, o)
                wait(dve, scanned, i, o - 1)
                wait(dve, turned, i, o - RING)
                dve.tensor_tensor_scan(seg[:, b, 0:w], limit[:, b, 0:w], ps_msg[o % 2][:, 0:w],
                                       seg[:, (o - 1) % RING, CH - 1:CH], ALU.min, ALU.max).then_inc(scanned, 1)

            def windows():
                def step(i, off, peeled):
                    if there(off - 2, peeled):
                        o = off - 2
                        wait(dve, topped, i, o)
                        wait(dve, w_stored, i, o - RING, 16)
                        dve.scalar_tensor_tensor(out=w_top[:, o % RING, :], in0=b2_all[0:WIN, :],
                                                 scalar=ps_top[0:WIN, D:D + 1], in1=ps_top[0:WIN, 0:D],
                                                 op0=ALU.mult, op1=ALU.add).then_inc(w_top_made, 1)
                    if there(off + 3, peeled):
                        o = off + 3
                        nt = tiles(o, peeled)
                        wait(dve, spread, i, o)
                        wait(dve, summed, i, o - 2)
                        dve.tensor_scalar(pick[:, o % 2, 0:128 * nt].rearrange("n (t p) -> n t p", t=nt),
                                          ps_local[0:TALL, 0:128 * nt].rearrange("n (p t) -> n t p", t=nt),
                                          third[0:TALL, 0:1], None, ALU.is_equal).then_inc(picked, 1)
                    if there(off + 1, peeled):
                        scan(i, off + 1, tiles(off + 1, peeled))
                    if there(off, peeled):
                        o = off
                        b, nt = o % RING, tiles(o, peeled)
                        wait(dve, ends_in, i, o, 16)
                        wait(dve, topped, i, o - 2)
                        dve.tensor_tensor(chosen[:, o % 2, 0:nt, :],
                                          place[:, :].unsqueeze(1).broadcast_to([128, nt, WIN]),
                                          ends[:, b, 0:nt].unsqueeze(2).broadcast_to([128, nt, WIN]),
                                          ALU.is_equal).then_inc(chosen_made, 1)
                chunks(dve, step, ahead=3, behind=2)
                dve.wait_ge(x_again, 16 * (GROUPS // 2))

                def finish(i, h):
                    if is_group(i, h, 1):
                        center(i + h, 1 - h)
                    scale(i, h)

                center(0, 0)
                groups(dve, finish)

            def general():
                def step(i, off, peeled):
                    if there(off + 1, peeled):
                        scan(i, off + 1, tiles(off + 1, peeled))

                chunks(dve, step, ahead=3)
                dve.wait_ge(sample_in, 16)
                dve.tensor_copy(sample_f[:, :], sample_i[:, :]).then_inc(sample_cast, 1)
                dve.tensor_copy(node[:, :], node_i[:, :]).then_inc(node_cast, 1)
                dve.wait_ge(sample_spread, 1)
                dve.tensor_copy(sample_all[:, 0:512], ps_msg[0][0:NP, :])
                link(dve.tensor_copy(sample_all[:, 512:SAMPLES], ps_msg[1][0:NP, 0:SAMPLES - 512]))
                def samples_up_to(k):
                    freed(dve, coarse_made, k)
                    dve.tensor_scalar(junk[:, 0:SAMPLES], sample_all[:, :], node[:, bass.ds(k, 1)], 0.0, ALU.is_le, ALU.add,
                                      accum_out=coarse[:, bass.ds(k, 1)]).then_inc(coarse_made, 1)

                dve.wait_ge(node_cast, 1)
                samples_up_to(0)
                with dve.Fori(1, KB) as k:
                    samples_up_to(k)
                dve.wait_ge(coarse_made, KB)
                link(dve.tensor_scalar(span_f[:, :], coarse[:, :], -1.0, 0.0, ALU.add, ALU.max))
                def count(i, h):
                    dve.wait_ge(span_in[h], 16 * GROUP * (i + 1))
                    for k in range(GROUP):
                        freed(dve, fine_made, GROUP * (2 * i + h) + k)
                        at = bass.ds(GROUP * (2 * i + h) + k, 1)
                        low = span_rows[h][:, k, :].bitcast(I16).rearrange("n (j a) -> n j a", a=2)[:, :, 0]
                        dve.tensor_scalar(junk[:, :], low, node[:, at], 0.0, ALU.is_le, ALU.add,
                                          accum_out=fine[:, at]).then_inc(fine_made, 1)

                def name(i, h):
                    dve.tensor_copy(span_at[:, h, :], span_f[:, bass.ds(GROUP * (2 * i + h), GROUP)]).then_inc(span_named, 1)

                for h in range(2):
                    name(0, h)

                def count_and_name(i, h):
                    count(i, h)
                    dve.wait_ge(fine_made, GROUP * (2 * i + h + 1))
                    name(i + 1, h)

                turns(dve, KB // GROUP // 2 - 1, count_and_name)
                for h in range(2):
                    count(KB // GROUP // 2 - 1, h)
                dve.wait_ge(fine_made, KB)
                dve.scalar_tensor_tensor(out=end[:, :], in0=span_f[:, :], scalar=float(SPAN), in1=fine[:, :],
                                         op0=ALU.mult, op1=ALU.add).then_inc(end_made, 1)
                dve.wait_ge(end_made, 1)
                dve.tensor_scalar(last_f[:, :], end[:, :], -1.0, 0.0, ALU.add, ALU.max)
                dve.wait_ge(start_in, 16)
                link(dve.tensor_tensor(filled[:, :], end[:, :], start[:, :], ALU.is_gt))

                def name_last(i, h):
                    dve.tensor_copy(last_at[:, h, :], last_f[:, bass.ds(GROUP * (2 * i + h), GROUP)]).then_inc(last_named, 1)

                def finish(i, h):
                    n = 2 * i + h + 1
                    dve.wait_ge(top_in[h], 16 * GROUP * (i + 1))
                    dve.tensor_tensor(top[:, h, :, :], top[:, h, :, :],
                                      b2_all[:, :].unsqueeze(1).broadcast_to([NP, GROUP, D]), ALU.add).then_inc(top_b2, 1)
                    dve.wait_ge(top_b2, n)
                    dve.tensor_tensor(top[:, h, :, :], top[:, h, :, :],
                                      filled[:, bass.ds(GROUP * (2 * i + h), GROUP)].unsqueeze(2)
                                      .broadcast_to([NP, GROUP, D]), ALU.mult).then_inc(top_kept, 1)
                    dve.wait_ge(top_kept, n)
                    center(i, h)
                    if is_group(i, h, 2):
                        name_last(i + 1, h)
                    scale(i, h)

                for h in range(2):
                    name_last(0, h)
                dve.wait_ge(x_again, 16 * (GROUPS // 2))
                groups(dve, finish)

            either(dve, windows, general)


_INS = ["x", "src", "dst", "L0_gnn_W1", "L0_gnn_b1", "L0_gnn_W2", "L0_gnn_b2"]


def kernel(**inputs):
    import numpy as _np
    import concourse.bacc as _bacc
    from concourse.bass_utils import run_bass_kernel_spmd as _run

    nc = _bacc.Bacc("TRN2", target_bir_lowering=False, num_devices=1)
    arrays, args = {}, []
    for name in _INS:
        a = _np.ascontiguousarray(inputs[name])
        arrays[f"in_{name}_dram"] = a
        args.append(nc.dram_tensor(f"in_{name}_dram", a.shape, mybir.dt.from_np(a.dtype), kind="ExternalInput").ap())
    args.append(nc.dram_tensor("out_0_dram", inputs["x"].shape, F32, kind="ExternalOutput").ap())
    gnn_max_resnorm(nc, *args)
    return _run(nc, [arrays], core_ids=[0]).results[0]["out_0_dram"]
```

```python
from contextlib import ExitStack

import concourse.bass as bass
from concourse import mybir

F32 = mybir.dt.float32
BF16 = mybir.dt.bfloat16
I32 = mybir.dt.int32
U32 = mybir.dt.uint32
I16 = mybir.dt.int16
ALU = mybir.AluOpType
ACT = mybir.ActivationFunctionType
AX = mybir.AxisListType

RING = 4
HALF_BIG = 255.0 * 2.0 ** 119
EPS = 1e-5


def gnn_max_resnorm(nc, x, src, dst, W1, b1, W2, b2, out):
    N, D = x.shape
    E = src.shape[0]

    NP = 125
    KB = N // NP
    assert N == NP * KB and D == 128
    T = 4
    CH = 128 * T
    NC = -(-E // CH)
    LAST = (E - (NC - 1) * CH) // 128
    assert E % 128 == 0 and 1 <= LAST <= T
    FOUR = 4
    AHEAD = 4
    FOURS = KB // FOUR
    GROUP = 5
    assert FOURS % AHEAD == 1 and KB % (2 * GROUP) == 0
    GROUPS = KB // GROUP
    assert GROUPS % RING == 0
    PARTS = 3
    WIN = 128 // PARTS
    TALL = PARTS * WIN
    SPAN = 640
    SAMPLES = E // SPAN
    assert SAMPLES * SPAN == E
    G = -(-NC // 128)
    GF = (NC - 1) // 128
    QF = NC - 1 - 128 * GF

    with ExitStack() as ctx:
        def sb(name, shape, dt=F32):
            return ctx.enter_context(nc.sbuf_tensor(name, shape, dt))

        def ps(name):
            return ctx.enter_context(nc.psum_tensor(name, [128, 512], F32))

        def sem(name):
            return ctx.enter_context(nc.semaphore(name))

        def sems(name, n=RING):
            return [sem(f"{name}{i}") for i in range(n)]

        def dram(name, shape, dt=F32):
            return nc.dram_tensor(name, shape, dt, kind="Internal").ap()

        q_tab = dram("q_tab", [N, D])
        p_tab = dram("p_tab", [N + WIN, PARTS * D], BF16)
        top_tab = dram("top_tab", [N + WIN, D])
        seg_tab = dram("seg_tab", [E, D])
        row_tab = dram("row_tab", [NC, 2 * CH], BF16)
        ends_tab = dram("ends_tab", [NC, CH])
        base_tab = dram("base_tab", [NC, 1], I32)
        flag_tab = dram("flag_tab", [1, 1], I32)
        end_tab = dram("end_tab", [N + 1])

        ident = sb("ident", [128, 128])
        ident_bf = sb("ident_bf", [128, 128], BF16)
        lane_i = sb("lane_i", [128, 1], I32)
        lane = sb("lane", [128, 1])
        place_i = sb("place_i", [128, WIN], I32)
        place = sb("place", [128, WIN])
        thirds = sb("thirds", [128, WIN])
        third = sb("third", [128, 1])
        pad = sb("pad", [WIN, PARTS * D], BF16)
        node_i = sb("node_i", [NP, KB], I32)
        node = sb("node", [NP, KB])
        ones_row = sb("ones_row", [1, 128])
        ones_bf = sb("ones_bf", [1, 128], BF16)
        zero1 = sb("zero1", [1, 1])
        eps = sb("eps", [128, 1])
        w1 = sb("w1", [D, 2, D])
        w_qp = sb("w_qp", [D, 2, D])
        w2 = sb("w2", [D, D])
        b1_col = sb("b1_col", [D, 1])
        b2_all = sb("b2_all", [NP, D])
        x_in = sb("x_in", [NP, AHEAD, FOUR, D])
        x_t = sb("x_t", [D, 2, FOUR, NP])
        p_out = sb("p_out", [NP, AHEAD, FOUR, D])
        p_rest = sb("p_rest", [NP, FOUR, D])
        room = sb("room", [128, 4, G, CH])
        x_all = room[0:NP].rearrange("n r g j -> n (r g j)")[:, 0:KB * D].rearrange("n (k f) -> n k f", k=KB)
        dst_f, edge_f, dst_c = room[:, 0], room[:, 1], room[:, 2].bitcast(I32)
        prev_c = sb("prev_c", [128, G], I32)
        prev_f = sb("prev_f", [128, G])
        next_c = sb("next_c", [128, G], I32)
        next_f = sb("next_f", [128, G])
        row_c = sb("row_c", [128, G, 2, CH], BF16)
        base_f = sb("base_f", [128, G])
        base_i = sb("base_i", [128, G], I32)
        gap = sb("gap", [128, 2, G])
        far = sb("far", [128, 1])
        far1 = sb("far1", [1, 1])
        far_i = sb("far_i", [1, 1], I32)
        sample_i = sb("sample_i", [1, SAMPLES], I32)
        sample_f = sb("sample_f", [1, SAMPLES])
        sample_all = sb("sample_all", [NP, SAMPLES])
        junk = sb("junk", [NP, SPAN], BF16)
        coarse = sb("coarse", [NP, KB])
        span_f = sb("span_f", [NP, KB])
        span_at = sb("span_at", [NP, 2, GROUP], U32)
        span_more = sb("span_more", [NP, GROUP, SPAN], I32)
        span_rows = [row_c[0:NP].rearrange("n g a j -> n (g a j)")[:, 0:2 * GROUP * SPAN].bitcast(I32)
                     .rearrange("n (k j) -> n k j", k=GROUP), span_more]
        fine = sb("fine", [NP, KB])
        end = sb("end", [NP, KB])
        start = sb("start", [NP, KB])
        filled = sb("filled", [NP, KB])
        last_f = sb("last_f", [NP, KB])
        idx = sb("idx", [128, RING, T], I32)
        idx_d = sb("idx_d", [128, RING, T], I32)
        rows = sb("rows", [1, RING, 2, CH], BF16)
        win = sb("win", [TALL, RING, D], BF16)
        q_rows = sb("q_rows", [128, RING, T, D])
        p_rows = sb("p_rows", [128, RING, T, PARTS * D], BF16)
        pick = sb("pick", [TALL, 2, CH], BF16)
        ends = sb("ends", [128, RING, T])
        limit = sb("limit", [128, RING, CH])
        assert AHEAD == RING and FOUR == T
        q_out = limit[0:NP].rearrange("n s (k f) -> n s k f", k=FOUR)
        p_parts = p_rows[0:NP].rearrange("n s k (a f) -> n s k a f", a=PARTS)
        hid = sb("hid", [D, 2, CH])
        seg = sb("seg", [D, RING, CH])
        seg_t = sb("seg_t", [128, 2, T, D + 1])
        chosen = sb("chosen", [128, 2, T, WIN])
        w_top = sb("w_top", [WIN, RING, D])
        last_at = sb("last_at", [NP, RING, GROUP], U32)
        top = p_rows[0:NP].rearrange("n s t f -> n (s t f)").bitcast(F32)[:, 0:RING * GROUP * D].rearrange(
            "n (s k f) -> n s k f", s=RING, k=GROUP)
        fin = row_c[0:NP].rearrange("n g a j -> n (g a j)").bitcast(F32)[:, 0:RING * GROUP * D].rearrange(
            "n (s k f) -> n s k f", s=RING, k=GROUP)
        res = sb("res", [NP, RING, GROUP, D])
        stats = sb("stats", [NP, RING, GROUP, 6])
        mv = sb("mv", [NP, RING, GROUP, 2])
        std = sb("std", [NP, RING, GROUP, 1])
        rstd = sb("rstd", [NP, RING, GROUP, 1])
        shift = sb("shift", [NP, RING, GROUP, 1])

        ps_local = ps("ps_local")
        ps_limit = ps("ps_limit")
        ps_hid = [ps("ps_hid0"), ps("ps_hid1")]
        ps_msg = [ps("ps_msg0"), ps("ps_msg1")]
        ps_seg = ps("ps_seg")
        ps_top = ps("ps_top")

        ident_zeroed, ident_made, iota_made, const_made = (sem("ident_zeroed"), sem("ident_made"),
                                                           sem("iota_made"), sem("const_made"))
        w1_in, w2_in, b1_in, b2_in, w_made = sem("w1_in"), sem("w2_in"), sem("b1_in"), sem("b2_in"), sem("w_made")
        ones_col_made = sem("ones_col_made")
        x_loaded = sems("x_loaded", AHEAD)
        xt_made, xt_copied, qp_made = sem("xt_made"), sem("xt_copied"), sem("qp_made")
        qp_copied, q_stored, p_stored = sem("qp_copied"), sems("q_stored", AHEAD), sems("p_stored", AHEAD)
        part_made, pad_made, pad_stored, ident_bf_made = (sem("part_made"), sem("pad_made"), sem("pad_stored"),
                                                          sem("ident_bf_made"))
        dst_filled, dst_in, near_in, sample_in = sem("dst_filled"), sem("dst_in"), sem("near_in"), sem("sample_in")
        dve_step = sem("dve_step")
        rows_made, rows_stored, ends_stored = sem("rows_made"), sem("rows_stored"), sem("ends_stored")
        last_marked, dst_cast, local_made, same_made = (sem("last_marked"), sem("dst_cast"), sem("local_made"),
                                                        sem("same_made"))
        base_made, base_stored = sem("base_made"), sem("base_stored")
        far_made, far_turned, flag_made, flag_stored = (sem("far_made"), sem("far_turned"), sem("flag_made"),
                                                        sem("flag_stored"))
        node_cast = sem("node_cast")
        sample_cast, sample_spread, coarse_made = sem("sample_cast"), sem("sample_spread"), sem("coarse_made")
        span_named, span_in, fine_made = sem("span_named"), sems("span_in", 2), sem("fine_made")
        zero_stored, end_made, end_stored, start_in = (sem("zero_stored"), sem("end_made"), sem("end_stored"),
                                                       sem("start_in"))

        idx_in, rows_in, win_in, gathered = sems("idx_in"), sems("rows_in"), sems("win_in"), sems("gathered")
        spread, picked, limit_copied = sem("spread"), sem("picked"), sem("limit_copied")
        summed, relued, product, scanned = sem("summed"), sem("relued"), sem("product"), sem("scanned")
        turned, turned_copied, seg_stored = sem("turned"), sem("turned_copied"), sems("seg_stored")
        ends_in, chosen_made, topped = sems("ends_in"), sem("chosen_made"), sem("topped")
        w_top_made = sem("w_top_made")
        w_stored = sems("w_stored")

        last_named, top_in, x_again = sem("last_named"), sems("top_in"), sem("x_again")
        top_b2, top_kept, res_made, stats_made, mv_made = (sem("top_b2"), sem("top_kept"), sem("res_made"),
                                                           sem("stats_made"), sem("mv_made"))
        std_made, rstd_made, shift_made, fin_made = (sem("std_made"), sem("rstd_made"), sem("shift_made"),
                                                     sem("fin_made"))
        out_stored = sems("out_stored")

        ctx.enter_context(nc.allow_non_contiguous_dma(reason="one dst for each chunk or span"))
        passed = sem("passed")

        block = ctx.enter_context(nc.Block())

        def wait(eng, stage, i, off, by=1):
            if isinstance(stage, list):
                stage, value = stage[off % RING], (i + off // RING + 1) * by
            else:
                value = RING * i + off + 1
            freed(eng, stage, value)

        def tiles(off, peeled):
            return LAST if peeled and off == NC - 1 else T

        def chunks(eng, step, ahead=0, behind=0, rings=1):
            turn = rings * RING
            loops = (NC - RING) // turn
            for s in range(-ahead, turn):
                step(0, s, True)
            with eng.Fori(1, loops) as i:
                for off in range(turn):
                    step(i if rings == 1 else i * rings, off, False)
            for s in range(loops * turn, NC + behind):
                step(0, s, True)

        def turns(eng, n, body):
            for h in range(2):
                body(0, h)
            with eng.Fori(1, n) as i:
                for h in range(2):
                    body(i, h)

        def freed(eng, semaphore, value):
            if not isinstance(value, int) or value > 0:
                eng.wait_ge(semaphore, value)

        def fours(eng, body):
            for h in range(AHEAD):
                body(0, h)
            with eng.Fori(1, FOURS // AHEAD) as i:
                for h in range(AHEAD):
                    body(i, h)
            body(FOURS // AHEAD, 0)

        def whole(eng, stored):
            for h in range(AHEAD):
                eng.wait_ge(stored[h], 16 * (FOURS // AHEAD + (h < FOURS % AHEAD)))

        def groups(eng, step):
            for h in range(RING):
                step(0, h)
            with eng.Fori(1, GROUPS // RING - 1) as i:
                for h in range(RING):
                    step(i, h)
            for h in range(RING):
                step(GROUPS // RING - 1, h)

        def behind(i, h):
            return (i, h + 1) if h + 1 < RING else (i + 1, 0)

        def is_group(i, h, ahead=0):
            return not isinstance(i, int) or RING * i + h + ahead < GROUPS

        def there(off, peeled):
            return not peeled or 0 <= off < NC

        def either(eng, windows, general):
            eng.wait_ge(flag_stored, 16)
            flag = eng.value_load(flag_tab[0:1, 0:1], min_val=0, max_val=1)
            with eng.If(flag == 0):
                windows()
            with eng.Else():
                general()

        def apart(eng):
            eng.sem_inc(passed, 1)

        def chunk_rows(table, tile):
            return ((table[0:GF * 128].rearrange("(g q) j -> q g j", q=128), tile[:, 0:GF, :]),
                    (table[GF * 128:NC], tile[0:QF + 1, GF, :]))

        def blocks_of(table):
            return table.rearrange("(p k) f -> p k f", k=KB)

        @block.sync
        def _(sp):
            def load_x(i, h):
                freed(sp, xt_made, AHEAD * (i - 1) + h + 1)
                sp.dma_start(x_in[:, h, :, :],
                             blocks_of(x)[:, bass.ds(FOUR * (AHEAD * i + h), FOUR), :]).then_inc(x_loaded[h], 16)

            def store_qp(i, h):
                n = AHEAD * i + h
                at = bass.ds(FOUR * n, FOUR)
                sp.wait_ge(qp_copied, 2 * (n + 1))
                sp.dma_start(blocks_of(q_tab)[:, at, :], q_out[:, h, :, :]).then_inc(q_stored[h], 16)
                sp.wait_ge(part_made, PARTS * (n + 1))
                sp.dma_start(blocks_of(p_tab[0:N])[:, at, :],
                             p_parts[:, h, :, :, :].rearrange("n k a f -> n k (a f)")).then_inc(p_stored[h], 16)

            load_x(0, 0)
            sp.dma_start(w1[:, :, :], W1.rearrange("(a f) o -> f a o", a=2)).then_inc(w1_in, 16)
            for h in range(1, AHEAD):
                load_x(0, h)
            sp.wait_ge(dst_filled, 3)
            sp.dma_start(dst_c[:, 0:GF, :],
                         dst[0:GF * 128 * CH].rearrange("(g q j) -> q g j", q=128, j=CH)).then_inc(dst_in, 16)
            sp.dma_start(dst_c[0:QF, GF, :],
                         dst[GF * 128 * CH:(NC - 1) * CH].rearrange("(q j) -> q j", j=CH)).then_inc(dst_in, 16)
            sp.dma_start(dst_c[QF:QF + 1, GF, 0:LAST * 128],
                         dst[(NC - 1) * CH:E].rearrange("(q j) -> q j", q=1)).then_inc(dst_in, 16)
            def load_idx(i, off, peeled):
                b, nt = off % RING, tiles(off, peeled)
                wait(sp, gathered, i, off - RING, 16 * T)
                sp.dma_start(idx[:, b, 0:nt], src[bass.ds(CH * RING * i + CH * off, 128 * nt)]
                             .rearrange("(p t) -> p t", t=nt)).then_inc(idx_in[b], 16)

            def products(i, h):
                if h == 0 or not isinstance(i, int) or i + 1 < FOURS // AHEAD:
                    load_x(i + 1, h)
                store_qp(i, h)

            for h in range(AHEAD):
                products(0, h)
            for c in range(RING):
                load_idx(0, c, True)
            sp.dma_start(w2[:, :], W2).then_inc(w2_in, 16)
            sp.dma_start(b1_col[:, :], b1.rearrange("(f a) -> f a", a=1)).then_inc(b1_in, 16)
            sp.dma_start(b2_all[:, :], b2.partition_broadcast(NP)).then_inc(b2_in, 16)
            with sp.Fori(1, FOURS // AHEAD - 1) as i:
                for h in range(AHEAD):
                    products(i, h)
            for h in range(AHEAD):
                products(FOURS // AHEAD - 1, h)
            store_qp(FOURS // AHEAD, 0)
            sp.wait_ge(pad_made, 1)
            sp.dma_start(p_tab[N:N + WIN, :], pad[:, :]).then_inc(pad_stored, 16)
            sp.wait_ge(flag_made, 1)
            sp.dma_start(flag_tab[:, :], far_i[:, :]).then_inc(flag_stored, 16)
            sp.wait_ge(base_made, 1)
            for to, of in chunk_rows(base_tab, base_i[:, :].unsqueeze(2)):
                sp.dma_start(to, of).then_inc(base_stored, 16)
            sp.wait_ge(rows_made, 1)
            sp.wait_ge(local_made, 1)
            for to, of in chunk_rows(row_tab, row_c[:, :, :, :].rearrange("q g n j -> q g (n j)")):
                sp.dma_start(to, of).then_inc(rows_stored, 16)
            sp.wait_ge(rows_made, 2)
            for to, of in chunk_rows(ends_tab, edge_f):
                sp.dma_start(to, of).then_inc(ends_stored, 16)
            sp.wait_ge(rows_stored, 32)
            sp.wait_ge(base_stored, 32)
            sp.wait_ge(pad_stored, 16)
            whole(sp, q_stored)
            whole(sp, p_stored)

            def load_part_of_x(part):
                at = slice(2 * GROUP * part, 2 * GROUP * (part + 1))
                sp.dma_start(x_all[:, at, :], blocks_of(x)[:, at, :]).then_inc(x_again, 16)

            def store_out(i, h):
                sp.wait_ge(fin_made, RING * i + h + 1)
                sp.dma_start(blocks_of(out)[:, bass.ds(GROUP * (RING * i + h), GROUP), :],
                             fin[:, h, :, :]).then_inc(out_stored[h], 16)

            def load(i, off, peeled, general):
                b, nt = off % RING, tiles(off, peeled)
                if general:
                    wait(sp, gathered, i, off - RING, 2 * 16 * T)
                    sp.dma_start(idx_d[:, b, 0:nt], dst[bass.ds(CH * RING * i + CH * off, 128 * nt)]
                                 .rearrange("(p t) -> p t", t=nt)).then_inc(idx_in[b], 16)
                if not peeled or off >= RING:
                    load_idx(i, off, peeled)
                wait(sp, spread, i, off - RING)
                sp.dma_start(rows[:, b, :, :], row_tab[bass.ds(RING * i + off, 1), :]
                             .rearrange("a (n j) -> a n j", n=2)).then_inc(rows_in[b], 16)

            def windows():
                def step(i, off, peeled):
                    if there(off + RING, peeled):
                        load(i, off + RING, peeled, False)
                        o = off + RING
                        b = o % RING
                        first = sp.value_load(base_tab[bass.ds(RING * i + o, 1), 0:1], min_val=0, max_val=N - 1)
                        wait(sp, summed, i, o - RING)
                        sp.dma_start(win[:, b, :], p_tab[bass.ds(first, WIN), :]
                                     .rearrange("n (a f) -> (n a) f", a=PARTS)).then_inc(win_in[b], 16)
                    if peeled and off == -2:
                        sp.wait_ge(ends_stored, 32)
                    if there(off + 2, peeled):
                        o = off + 2
                        b, nt = o % RING, tiles(o, peeled)
                        wait(sp, chosen_made, i, o - RING)
                        sp.dma_start(ends[:, b, 0:nt],
                                     ends_tab[bass.ds(RING * i + o, 1), 0:128 * nt]
                                     .rearrange("a (p t) -> (a p) t", t=nt)).then_inc(ends_in[b], 16)
                    if peeled and 0 <= off < GROUPS // 2:
                        load_part_of_x(off)

                chunks(sp, step, ahead=RING, rings=4)
                for c in range(NC - RING, NC):
                    wait(sp, w_stored, 0, c, 16)

                def load_top(i, h):
                    freed(sp, res_made, RING * (i - 1) + h + 1)
                    sp.dma_start(top[:, h, :, :], blocks_of(top_tab[0:N])[:, bass.ds(GROUP * (RING * i + h), GROUP), :]
                                 ).then_inc(top_in[h], 16)

                for h in range(RING):
                    load_top(0, h)

                def finish(i, h):
                    if is_group(i, h, RING):
                        load_top(i + 1, h)
                    store_out(i, h)

                groups(sp, finish)

            def general():
                def step(i, off, peeled):
                    if there(off + RING, peeled):
                        load(i, off + RING, peeled, True)
                    if there(off, peeled):
                        b, nt = off % RING, tiles(off, peeled)
                        wait(sp, turned_copied, i, off)
                        sp.dma_start(seg_tab[bass.ds(CH * RING * i + CH * off, 128 * nt), :]
                                     .rearrange("(p t) f -> p t f", t=nt),
                                     seg_t[:, off % 2, 0:nt, 0:D]).then_inc(seg_stored[b], 16)

                sp.wait_ge(ends_stored, 32)
                for part in range(GROUPS // 2):
                    load_part_of_x(part)
                chunks(sp, step, ahead=RING)
                sp.dma_start(sample_i[:, :],
                             dst.rearrange("(a s j) -> a s j", a=1, j=SPAN)[:, :, 0]).then_inc(sample_in, 16)
                sp.dma_start(end_tab[0:1].rearrange("(a b) -> a b", a=1), zero1[:, :]).then_inc(zero_stored, 16)
                sp.wait_ge(end_made, 1)
                sp.dma_start(end_tab[1:N + 1].rearrange("(p k) -> p k", k=KB), end[:, :]).then_inc(end_stored, 16)
                sp.wait_ge(end_stored, 16)
                sp.wait_ge(zero_stored, 16)
                sp.dma_start(start[:, :], end_tab[0:N].rearrange("(p k) -> p k", k=KB)).then_inc(start_in, 16)

                groups(sp, store_out)

            either(sp, windows, general)
            for h in range(RING):
                sp.wait_ge(out_stored[h], 16 * (GROUPS // RING))

        @block.gpsimd
        def _(pool):
            pool.memset(dst_c[:, GF, :], -1).then_inc(dst_filled, 1)
            pool.memset(prev_c[:, :], -1).then_inc(dst_filled, 1)
            pool.memset(next_c[:, :], -1).then_inc(last_marked, 1)
            pool.wait_ge(last_marked, 1)
            pool.affine_select(out=next_c[:, GF:G], in_=next_c[:, GF:G], compare_op=ALU.not_equal, fill=N,
                               base=-QF, pattern=[[0, 1]], channel_multiplier=1).then_inc(dst_filled, 1)
            pool.memset(ident[:, :], 0.0).then_inc(ident_zeroed, 1)
            pool.wait_ge(ident_zeroed, 1)
            pool.affine_select(out=ident[:, :], in_=ident[:, :], compare_op=ALU.not_equal, fill=1.0, base=0,
                               pattern=[[-1, 128]], channel_multiplier=1).then_inc(ident_made, 1)
            pool.iota(lane_i[:, :], pattern=[[0, 1]], base=0, channel_multiplier=1).then_inc(iota_made, 1)
            pool.iota(place_i[:, :], pattern=[[1, WIN]], base=1, channel_multiplier=0).then_inc(iota_made, 1)
            pool.iota(node_i[:, :], pattern=[[1, KB]], base=0, channel_multiplier=KB).then_inc(iota_made, 1)

            pool.memset(pad[:, :], 0.0).then_inc(pad_made, 1)
            pool.wait_ge(dst_filled, 3)
            each = dst.rearrange("(e a) -> e a", a=1)
            for g in range(G):
                lo, n = (1 if g == 0 else 0), (128 if g < GF else QF + 1)
                first = (128 * g + lo) * CH - 1
                pool.dma_start(prev_c[lo:n, g:g + 1],
                             each[first:first + (n - lo - 1) * CH + 1:CH, :]).then_inc(near_in, 16)
                n = 128 if g < GF else QF
                first = (128 * g + 1) * CH
                pool.dma_start(next_c[0:n, g:g + 1],
                             each[first:first + (n - 1) * CH + 1:CH, :]).then_inc(near_in, 16)
            pool.wait_ge(dst_cast, 1)
            pool.tensor_tensor(row_c[:, :, 1, :], dst_f[:, :, :],
                               base_f[:, :].unsqueeze(2).broadcast_to([128, G, CH]), ALU.subtract).then_inc(local_made, 1)
            pool.wait_ge(ident_made, 1)
            pool.tensor_copy(ident_bf[:, :], ident[:, :]).then_inc(ident_bf_made, 1)

            whole(pool, q_stored)

            def gather(i, off, peeled, rows_of, table, at):
                b = off % RING
                for t in range(tiles(off, peeled)):
                    pool.indirect_dma_start(
                        out=rows_of[:, b, t, :], out_offset=None, in_=table,
                        in_offset=bass.IndirectOffsetOnAxis(ap=at[:, b, t:t + 1].bitcast(U32), axis=0)
                    ).then_inc(gathered[b], 16)

            for c in range(RING):
                wait(pool, idx_in, 0, c, 16)
                gather(0, c, True, q_rows, q_tab, idx)

            def gathers(general):
                def step(i, off, peeled):
                    early = peeled and off < RING
                    if general or not early:
                        wait(pool, idx_in, i, off, 32 if general else 16)
                        wait(pool, summed, i, off - RING)
                        apart(pool)
                    if not early:
                        gather(i, off, peeled, q_rows, q_tab, idx)
                    if general:
                        gather(i, off, peeled, p_rows, p_tab[0:N], idx_d)

                chunks(pool, step, rings=4)

            def general():
                whole(pool, p_stored)
                gathers(True)
                spans = dst.rearrange("(s j) -> s j", j=SPAN)

                def fetch_spans(i, h):
                    pool.wait_ge(span_named, 2 * i + h + 1)
                    apart(pool)
                    for k in range(GROUP):
                        pool.indirect_dma_start(
                            out=span_rows[h][:, k, :], out_offset=None, in_=spans,
                            in_offset=bass.IndirectOffsetOnAxis(ap=span_at[:, h, k:k + 1], axis=0)
                        ).then_inc(span_in[h], 16)

                turns(pool, KB // GROUP // 2, fetch_spans)
                for c in range(NC - RING, NC):
                    wait(pool, seg_stored, 0, c, 16)

                def fetch_tops(i, h):
                    pool.wait_ge(last_named, RING * i + h + 1)
                    apart(pool)
                    for k in range(GROUP):
                        pool.indirect_dma_start(
                            out=top[:, h, k, :], out_offset=None, in_=seg_tab,
                            in_offset=bass.IndirectOffsetOnAxis(ap=last_at[:, h, k:k + 1], axis=0)
                        ).then_inc(top_in[h], 16)

                groups(pool, fetch_tops)

            def windows():
                gathers(False)
                pool.wait_ge(x_again, 16 * (GROUPS // 2))

                def add_x(i, h):
                    n = RING * i + h
                    pool.wait_ge(top_in[h], 16 * (i + 1))
                    freed(pool, fin_made, n - RING + 1)
                    pool.tensor_tensor(res[:, h, :, :], top[:, h, :, :], x_all[:, bass.ds(GROUP * n, GROUP), :],
                                       ALU.add).then_inc(res_made, 1)

                groups(pool, add_x)

            either(pool, windows, general)

        @block.scalar
        def _(act):
            def copy_turned(i, h):
                n, slot = AHEAD * i + h, h % 2
                act.wait_ge(xt_made, n + 1)
                freed(act, qp_made, 2 * (n - 1))
                act.activation(x_t[:, slot, :, :], ps_hid[slot][:, 0:FOUR * NP].rearrange("f (k n) -> f k n", k=FOUR),
                               ACT.Copy).then_inc(xt_copied, 1)

            def tables(i, h):
                n = AHEAD * i + h
                if h + 1 < AHEAD and (not isinstance(i, int) or i < FOURS // AHEAD):
                    copy_turned(i, h + 1)
                elif h + 1 == AHEAD:
                    copy_turned(i + 1, 0)
                freed(act, q_stored[h], 16 * i)
                freed(act, p_stored[h], 16 * i)
                for half in range(2):
                    blocks = slice(2 * half, 2 * half + 2)
                    from_ps = ps_msg[half][0:NP, :].rearrange("n (k a f) -> n k a f", k=2, a=2)
                    act.wait_ge(qp_made, 2 * n + half + 1)
                    act.activation(q_out[:, h, blocks, :], from_ps[:, :, 0, :], ACT.Copy)
                    act.activation(p_out[:, h, blocks, :], from_ps[:, :, 1, :], ACT.Copy)
                    act.activation(p_parts[:, h, blocks, 0, :], from_ps[:, :, 1, :], ACT.Copy).then_inc(qp_copied, 1)

            copy_turned(0, 0)
            fours(act, tables)
            act.wait_ge(b1_in, 16)

            def bounds(i, o):
                wait(act, spread, i, o)
                wait(act, scanned, i, o - RING)
                act.activation(limit[:, o % RING, :], ps_limit[:, :], ACT.Copy,
                               scale=2.0).then_inc(limit_copied, 1)

            def hidden(i, o, nt):
                wait(act, summed, i, o)
                wait(act, product, i, o - 2)
                act.activation(hid[:, o % 2, 0:128 * nt].rearrange("f (p t) -> f p t", t=nt),
                               ps_hid[o % 2][:, 0:128 * nt].rearrange("f (t p) -> f p t", t=nt),
                               ACT.Relu, bias=b1_col[:, 0:1]).then_inc(relued, 1)

            def turned_rows(i, o, nt):
                wait(act, turned, i, o)
                act.activation(seg_t[:, o % 2, 0:nt, 0:D],
                               ps_seg[:, 0:128 * nt].rearrange("p (t f) -> p t f", t=nt),
                               ACT.Copy).then_inc(turned_copied, 1)

            def windows():
                def step(i, off, peeled):
                    if there(off + 3, peeled):
                        bounds(i, off + 3)
                    if there(off + 2, peeled):
                        hidden(i, off + 2, tiles(off + 2, peeled))
                    if there(off, peeled):
                        wait(act, topped, i, off - 2)
                        turned_rows(i, off, tiles(off, peeled))
                    if there(off - 2, peeled):
                        o = off - 2
                        first = act.value_load(base_tab[bass.ds(RING * i + o, 1), 0:1], min_val=0, max_val=N - 1)
                        wait(act, w_top_made, i, o)
                        wait(act, w_stored, i, o - 1, 16)
                        act.dma_start(top_tab[bass.ds(first, WIN), :], w_top[:, o % RING, :]).then_inc(w_stored[o % RING], 16)

                chunks(act, step, ahead=3, behind=2)

            def general():
                def step(i, off, peeled):
                    if there(off + 3, peeled):
                        bounds(i, off + 3)
                    if there(off + 2, peeled):
                        hidden(i, off + 2, tiles(off + 2, peeled))
                    if there(off, peeled):
                        wait(act, seg_stored, i, off - 2, 16)
                        turned_rows(i, off, tiles(off, peeled))

                chunks(act, step, ahead=3)

            either(act, windows, general)

            def deviations(i, h):
                act.wait_ge(mv_made, RING * i + h + 1)
                act.activation(std[:, h, :, :], mv[:, h, :, 1:2], ACT.Sqrt, bias=eps[0:NP, 0:1]).then_inc(std_made, 1)

            def normalise(i, h):
                n = RING * i + h
                if is_group(i, h, 1):
                    deviations(*behind(i, h))
                act.wait_ge(shift_made, n + 1)
                freed(act, out_stored[h], 16 * i)
                for k in range(GROUP):
                    ins = act.activation(fin[:, h, k, :], res[:, h, k, :], ACT.Identity, bias=shift[:, h, k, :],
                                         scale=rstd[:, h, k, :])
                ins.then_inc(fin_made, 1)

            deviations(0, 0)
            groups(act, normalise)

        @block.tensor
        def _(pe):
            pe.wait_ge(ident_made, 1)

            def turn_x(i, h):
                pe.wait_ge(x_loaded[h], 16 * i + 16)
                freed(pe, xt_copied, AHEAD * i + h - 1)
                for k in range(FOUR):
                    mm = pe.transpose(ps_hid[h % 2][:, NP * k:NP * k + NP], x_in[:, h, k, :], ident[0:NP, 0:NP])
                mm.then_inc(xt_made, 1)

            def products(i, h):
                pe.wait_ge(xt_copied, AHEAD * i + h + 1)
                for half in range(2):
                    freed(pe, qp_copied, 2 * (AHEAD * i + h) + half - 1)
                    for k in range(2):
                        mm = pe.matmul(ps_msg[half][0:NP, 2 * D * k:2 * D * k + 2 * D], x_t[:, h % 2, 2 * half + k, :],
                                       w_qp[:, :, :].rearrange("f a o -> f (a o)"), start=True, stop=True)
                    mm.then_inc(qp_made, 1)

            turn_x(0, 0)
            pe.wait_ge(w_made, 2)

            def tables(i, h):
                turn_x(*((i, h + 1) if h + 1 < AHEAD else (i + 1, 0)))
                products(i, h)

            for h in range(AHEAD):
                tables(0, h)
            with pe.Fori(1, FOURS // AHEAD) as i:
                for h in range(AHEAD):
                    tables(i, h)
            products(FOURS // AHEAD, 0)

            pe.wait_ge(far_made, 1)
            pe.transpose(ps_top[0:1, 0:128], far[:, 0:1], ident[:, :]).then_inc(far_turned, 1)
            pe.wait_ge(w2_in, 16)
            pe.wait_ge(const_made, 4)
            pe.wait_ge(flag_made, 1)
            pe.wait_ge(qp_copied, 2 * FOURS)
            pe.wait_ge(flag_made, 1)

            def spread_rows(i, o, general):
                wait(pe, rows_in, i, o, 16)
                if not general:
                    wait(pe, picked, i, o - 1)
                    pe.matmul(ps_local[0:TALL, :], ones_bf[0:1, 0:TALL], rows[0:1, o % RING, 1, :], start=True, stop=True)
                wait(pe, limit_copied, i, o - 1)
                pe.matmul(ps_limit[:, :], ones_bf[0:1, :], rows[0:1, o % RING, 0, :],
                          start=True, stop=True).then_inc(spread, 1)

            def sum_up(i, o, peeled, general):
                b, nt = o % RING, tiles(o, peeled)
                wait(pe, relued, i, o - 2)
                if peeled and nt < T:
                    pe.wait_ge(gathered[b], 16 * (2 if general else 1) * (T * (o // RING) + nt))
                else:
                    wait(pe, gathered, i, o, 16 * T * (2 if general else 1))
                for t in range(nt):
                    pe.matmul(ps_hid[o % 2][:, 128 * t:128 * t + 128], q_rows[:, b, t, :], ident[:, :],
                              start=(t == 0), stop=False, is_transpose=True, skip_group_check=True)
                if general:
                    for t in range(nt):
                        for a in range(PARTS):
                            mm = pe.matmul(ps_hid[o % 2][:, 128 * t:128 * t + 128], p_rows[:, b, t, D * a:D * a + D],
                                           ident_bf[:, :], start=False, stop=(t == nt - 1 and a == PARTS - 1),
                                           skip_group_check=True)
                else:
                    wait(pe, win_in, i, o, 16)
                    wait(pe, picked, i, o)
                    mm = pe.matmul(ps_hid[o % 2][:, 0:128 * nt], win[:, b, :], pick[:, o % 2, 0:128 * nt],
                                   start=False, stop=True, skip_group_check=True)
                mm.then_inc(summed, 1)

            def message(i, o, nt):
                wait(pe, relued, i, o)
                wait(pe, scanned, i, o - 2)
                pe.matmul(ps_msg[o % 2][:, 0:128 * nt], w2[:, :], hid[:, o % 2, 0:128 * nt],
                          start=True, stop=True).then_inc(product, 1)

            def turn(i, o, nt):
                wait(pe, scanned, i, o)
                wait(pe, turned_copied, i, o - 1)
                for t in range(nt):
                    mm = pe.transpose(ps_seg[:, 128 * t:128 * t + 128], seg[:, o % RING, t:128 * nt:nt], ident[:, :])
                mm.then_inc(turned, 1)

            def windows():
                def step(i, off, peeled):
                    if there(off + 3, peeled):
                        spread_rows(i, off + 3, False)
                    if there(off + 2, peeled):
                        sum_up(i, off + 2, peeled, False)
                    if there(off + 1, peeled):
                        message(i, off + 1, tiles(off + 1, peeled))
                    if there(off, peeled):
                        turn(i, off, tiles(off, peeled))
                    if there(off - 1, peeled):
                        o = off - 1
                        nt = tiles(o, peeled)
                        wait(pe, turned_copied, i, o)
                        wait(pe, chosen_made, i, o)
                        wait(pe, w_top_made, i, o - 1)
                        for t in range(nt):
                            mm = pe.matmul(ps_top[0:WIN, 0:D + 1], chosen[:, o % 2, t, :], seg_t[:, o % 2, t, :],
                                           start=(t == 0), stop=(t == nt - 1))
                        mm.then_inc(topped, 1)

                pe.wait_ge(ones_col_made, 1)
                chunks(pe, step, ahead=3, behind=1)

            def general():
                pe.wait_ge(ident_bf_made, 1)

                def step(i, off, peeled):
                    if there(off + 3, peeled):
                        spread_rows(i, off + 3, True)
                    if there(off + 2, peeled):
                        sum_up(i, off + 2, peeled, True)
                    if there(off + 1, peeled):
                        message(i, off + 1, tiles(off + 1, peeled))
                    if there(off, peeled):
                        turn(i, off, tiles(off, peeled))

                chunks(pe, step, ahead=3)
                pe.wait_ge(sample_cast, 1)
                for h, (lo, n) in enumerate(((0, 512), (512, SAMPLES - 512))):
                    mm = pe.matmul(ps_msg[h][0:NP, 0:n], ones_row[0:1, 0:NP], sample_f[0:1, lo:lo + n],
                                   start=True, stop=True)
                mm.then_inc(sample_spread, 1)

            either(pe, windows, general)

        @block.vector
        def _(dve):
            steps = [0]

            def link(ins):
                steps[0] += 1
                ins.then_inc(dve_step, 1)
                dve.wait_ge(dve_step, steps[0])

            dve.wait_ge(w1_in, 16)
            dve.tensor_copy(w_qp[:, 0, :], w1[:, 1, :]).then_inc(w_made, 1)
            dve.tensor_tensor(w_qp[:, 1, :], w1[:, 0, :], w1[:, 1, :], ALU.subtract).then_inc(w_made, 1)
            dve.memset(ones_row[:, :], 1.0).then_inc(const_made, 1)
            dve.memset(ones_bf[:, :], 1.0).then_inc(const_made, 1)
            dve.memset(zero1[:, :], 0.0).then_inc(const_made, 1)
            dve.memset(eps[:, :], EPS).then_inc(const_made, 1)
            dve.memset(seg[:, RING - 1, CH - 1:CH], 0.0)
            dve.memset(seg_t[:, :, :, D:D + 1], 1.0).then_inc(ones_col_made, 1)
            dve.wait_ge(iota_made, 3)
            dve.tensor_copy(lane[:, :], lane_i[:, :])
            link(dve.tensor_copy(place[:, :], place_i[:, :]))
            link(dve.tensor_scalar(thirds[:, :], place[:, :], float(PARTS), lane[:, 0:1], ALU.mult, ALU.is_le))
            dve.tensor_reduce(third[:, :], thirds[:, :], AX.X, ALU.add)

            def split(i, h):
                n = AHEAD * i + h
                dve.wait_ge(qp_copied, 2 * n + 2)
                freed(dve, part_made, PARTS * n)
                dve.tensor_tensor(p_rest[:, :, :], p_out[:, h, :, :], p_parts[:, h, :, 0, :],
                                  ALU.subtract).then_inc(part_made, 1)
                dve.wait_ge(part_made, PARTS * n + 1)
                dve.tensor_copy(p_parts[:, h, :, 1, :], p_rest[:, :, :]).then_inc(part_made, 1)
                dve.wait_ge(part_made, PARTS * n + 2)
                dve.tensor_tensor(p_parts[:, h, :, 2, :], p_rest[:, :, :], p_parts[:, h, :, 1, :],
                                  ALU.subtract).then_inc(part_made, 1)

            for h in range(AHEAD):
                split(0, h)
            dve.wait_ge(dst_in, 48)
            dve.wait_ge(near_in, 32 * G)
            dve.tensor_copy(next_f[:, :], next_c[:, :])
            dve.tensor_copy(prev_f[:, :], prev_c[:, :])
            link(dve.tensor_copy(dst_f[:, :, :], dst_c[:, :, :]))
            link(dve.tensor_copy(base_f[:, :], dst_f[:, :, 0]))
            link(dve.memset(base_f[0:1, 0:1], 0.0))
            dve.tensor_copy(base_i[:, :], base_f[:, :]).then_inc(base_made, 1)
            dve.sem_inc(dst_cast, 1)
            dve.tensor_tensor(edge_f[:, :, 1:CH], dst_f[:, :, 1:CH], dst_f[:, :, 0:CH - 1], ALU.is_equal)
            dve.tensor_tensor(edge_f[:, :, 0], dst_f[:, :, 0], prev_f[:, :], ALU.is_equal).then_inc(same_made, 1)
            for h in range(AHEAD):
                split(1, h)
            dve.tensor_tensor(gap[:, 0, :], dst_f[:, :, CH - 1], base_f[:, :], ALU.subtract)
            link(dve.scalar_tensor_tensor(out=gap[:, 1, :], in0=next_f[:, :], scalar=-1.0, in1=base_f[:, :],
                                          op0=ALU.add, op1=ALU.subtract))
            dve.tensor_reduce(far[:, :], gap[:, :, :], AX.XY, ALU.max).then_inc(far_made, 1)
            with dve.Fori(2, FOURS // AHEAD) as i:
                for h in range(AHEAD):
                    split(i, h)
            split(FOURS // AHEAD, 0)
            dve.wait_ge(far_turned, 1)
            link(dve.tensor_reduce(far1[:, :], ps_top[0:1, 0:128], AX.X, ALU.max))
            dve.tensor_scalar(far_i[:, :], far1[:, :], float(WIN - 1), None, ALU.is_gt).then_inc(flag_made, 1)
            dve.wait_ge(same_made, 1)
            dve.tensor_scalar(row_c[:, :, 0, :], edge_f[:, :, :], -0.5, 2.0 * HALF_BIG,
                              ALU.add, ALU.mult).then_inc(rows_made, 1)
            dve.wait_ge(rows_made, 1)
            dve.wait_ge(local_made, 1)
            dve.tensor_tensor(edge_f[:, :, 0:CH - 1], dst_f[:, :, 0:CH - 1], dst_f[:, :, 1:CH], ALU.not_equal)
            link(dve.tensor_tensor(edge_f[:, :, CH - 1], dst_f[:, :, CH - 1], next_f[:, :], ALU.not_equal))
            dve.scalar_tensor_tensor(out=edge_f[:, :, :], in0=row_c[:, :, 1, :], scalar=1.0, in1=edge_f[:, :, :],
                                     op0=ALU.add, op1=ALU.mult).then_inc(rows_made, 1)
            dve.wait_ge(b2_in, 16)

            def center(i, h):
                n = RING * i + h
                dve.wait_ge(res_made, n + 1)
                for k in range(GROUP):
                    dve.bn_stats(stats[:, h, k, :], res[:, h, k, :]).then_inc(stats_made, 1)
                dve.wait_ge(stats_made, GROUP * (n + 1))
                apart(dve)
                for k in range(GROUP):
                    ins = dve.bn_aggr(mv[:, h, k, :], stats[:, h, k, :])
                ins.then_inc(mv_made, 1)

            def scale(i, h):
                n = RING * i + h
                dve.wait_ge(std_made, n + 1)
                dve.reciprocal(rstd[:, h, :, :], std[:, h, :, :]).then_inc(rstd_made, 1)
                dve.wait_ge(rstd_made, n + 1)
                dve.scalar_tensor_tensor(out=shift[:, h, :, :], in0=mv[:, h, :, 0:1], scalar=-1.0, in1=rstd[:, h, :, :],
                                         op0=ALU.mult, op1=ALU.mult).then_inc(shift_made, 1)

            def scan(i, o, nt):
                b, w = o % RING, 128 * nt
                wait(dve, product, i, o)
                wait(dve, limit_copied, i, o)
                wait(dve, scanned, i, o - 1)
                wait(dve, turned, i, o - RING)
                dve.tensor_tensor_scan(seg[:, b, 0:w], limit[:, b, 0:w], ps_msg[o % 2][:, 0:w],
                                       seg[:, (o - 1) % RING, CH - 1:CH], ALU.min, ALU.max).then_inc(scanned, 1)

            def windows():
                def step(i, off, peeled):
                    if there(off - 2, peeled):
                        o = off - 2
                        wait(dve, topped, i, o)
                        wait(dve, w_stored, i, o - RING, 16)
                        dve.scalar_tensor_tensor(out=w_top[:, o % RING, :], in0=b2_all[0:WIN, :],
                                                 scalar=ps_top[0:WIN, D:D + 1], in1=ps_top[0:WIN, 0:D],
                                                 op0=ALU.mult, op1=ALU.add).then_inc(w_top_made, 1)
                    if there(off + 3, peeled):
                        o = off + 3
                        nt = tiles(o, peeled)
                        wait(dve, spread, i, o)
                        wait(dve, summed, i, o - 2)
                        dve.tensor_scalar(pick[:, o % 2, 0:128 * nt].rearrange("n (t p) -> n t p", t=nt),
                                          ps_local[0:TALL, 0:128 * nt].rearrange("n (p t) -> n t p", t=nt),
                                          third[0:TALL, 0:1], None, ALU.is_equal).then_inc(picked, 1)
                    if there(off + 1, peeled):
                        scan(i, off + 1, tiles(off + 1, peeled))
                    if there(off, peeled):
                        o = off
                        b, nt = o % RING, tiles(o, peeled)
                        wait(dve, ends_in, i, o, 16)
                        wait(dve, topped, i, o - 2)
                        dve.tensor_tensor(chosen[:, o % 2, 0:nt, :],
                                          place[:, :].unsqueeze(1).broadcast_to([128, nt, WIN]),
                                          ends[:, b, 0:nt].unsqueeze(2).broadcast_to([128, nt, WIN]),
                                          ALU.is_equal).then_inc(chosen_made, 1)
                chunks(dve, step, ahead=3, behind=2)

                def finish(i, h):
                    if is_group(i, h, 1):
                        center(*behind(i, h))
                    scale(i, h)

                center(0, 0)
                groups(dve, finish)

            def general():
                def step(i, off, peeled):
                    if there(off + 1, peeled):
                        scan(i, off + 1, tiles(off + 1, peeled))

                chunks(dve, step, ahead=3)
                dve.wait_ge(sample_in, 16)
                dve.tensor_copy(sample_f[:, :], sample_i[:, :]).then_inc(sample_cast, 1)
                dve.tensor_copy(node[:, :], node_i[:, :]).then_inc(node_cast, 1)
                dve.wait_ge(sample_spread, 1)
                dve.tensor_copy(sample_all[:, 0:512], ps_msg[0][0:NP, :])
                link(dve.tensor_copy(sample_all[:, 512:SAMPLES], ps_msg[1][0:NP, 0:SAMPLES - 512]))
                def samples_up_to(k):
                    freed(dve, coarse_made, k)
                    dve.tensor_scalar(junk[:, 0:SAMPLES], sample_all[:, :], node[:, bass.ds(k, 1)], 0.0, ALU.is_le, ALU.add,
                                      accum_out=coarse[:, bass.ds(k, 1)]).then_inc(coarse_made, 1)

                dve.wait_ge(node_cast, 1)
                samples_up_to(0)
                with dve.Fori(1, KB) as k:
                    samples_up_to(k)
                dve.wait_ge(coarse_made, KB)
                link(dve.tensor_scalar(span_f[:, :], coarse[:, :], -1.0, 0.0, ALU.add, ALU.max))
                def count(i, h):
                    dve.wait_ge(span_in[h], 16 * GROUP * (i + 1))
                    for k in range(GROUP):
                        freed(dve, fine_made, GROUP * (2 * i + h) + k)
                        at = bass.ds(GROUP * (2 * i + h) + k, 1)
                        low = span_rows[h][:, k, :].bitcast(I16).rearrange("n (j a) -> n j a", a=2)[:, :, 0]
                        dve.tensor_scalar(junk[:, :], low, node[:, at], 0.0, ALU.is_le, ALU.add,
                                          accum_out=fine[:, at]).then_inc(fine_made, 1)

                def name(i, h):
                    dve.tensor_copy(span_at[:, h, :], span_f[:, bass.ds(GROUP * (2 * i + h), GROUP)]).then_inc(span_named, 1)

                for h in range(2):
                    name(0, h)

                def count_and_name(i, h):
                    count(i, h)
                    dve.wait_ge(fine_made, GROUP * (2 * i + h + 1))
                    name(i + 1, h)

                turns(dve, KB // GROUP // 2 - 1, count_and_name)
                for h in range(2):
                    count(KB // GROUP // 2 - 1, h)
                dve.wait_ge(fine_made, KB)
                dve.scalar_tensor_tensor(out=end[:, :], in0=span_f[:, :], scalar=float(SPAN), in1=fine[:, :],
                                         op0=ALU.mult, op1=ALU.add).then_inc(end_made, 1)
                dve.wait_ge(end_made, 1)
                dve.tensor_scalar(last_f[:, :], end[:, :], -1.0, 0.0, ALU.add, ALU.max)
                dve.wait_ge(start_in, 16)
                link(dve.tensor_tensor(filled[:, :], end[:, :], start[:, :], ALU.is_gt))

                def name_last(i, h):
                    dve.tensor_copy(last_at[:, h, :], last_f[:, bass.ds(GROUP * (RING * i + h), GROUP)]).then_inc(last_named, 1)

                def finish(i, h):
                    n = RING * i + h + 1
                    dve.wait_ge(top_in[h], 16 * GROUP * (i + 1))
                    dve.tensor_tensor(top[:, h, :, :], top[:, h, :, :],
                                      b2_all[:, :].unsqueeze(1).broadcast_to([NP, GROUP, D]), ALU.add).then_inc(top_b2, 1)
                    dve.wait_ge(top_b2, n)
                    dve.tensor_tensor(top[:, h, :, :], top[:, h, :, :],
                                      filled[:, bass.ds(GROUP * (RING * i + h), GROUP)].unsqueeze(2)
                                      .broadcast_to([NP, GROUP, D]), ALU.mult).then_inc(top_kept, 1)
                    dve.wait_ge(top_kept, n)
                    freed(dve, fin_made, n - RING)
                    dve.tensor_tensor(res[:, h, :, :], top[:, h, :, :], x_all[:, bass.ds(GROUP * (RING * i + h), GROUP), :],
                                      ALU.add).then_inc(res_made, 1)
                    center(i, h)
                    if is_group(i, h, RING):
                        name_last(i + 1, h)
                    scale(i, h)

                for h in range(RING):
                    name_last(0, h)
                dve.wait_ge(x_again, 16 * (GROUPS // 2))
                groups(dve, finish)

            either(dve, windows, general)


_INS = ["x", "src", "dst", "L0_gnn_W1", "L0_gnn_b1", "L0_gnn_W2", "L0_gnn_b2"]


def kernel(**inputs):
    import numpy as _np
    import concourse.bacc as _bacc
    from concourse.bass_utils import run_bass_kernel_spmd as _run

    nc = _bacc.Bacc("TRN2", target_bir_lowering=False, num_devices=1)
    arrays, args = {}, []
    for name in _INS:
        a = _np.ascontiguousarray(inputs[name])
        arrays[f"in_{name}_dram"] = a
        args.append(nc.dram_tensor(f"in_{name}_dram", a.shape, mybir.dt.from_np(a.dtype), kind="ExternalInput").ap())
    args.append(nc.dram_tensor("out_0_dram", inputs["x"].shape, F32, kind="ExternalOutput").ap())
    gnn_max_resnorm(nc, *args)
    return _run(nc, [arrays], core_ids=[0]).results[0]["out_0_dram"]
```
